# Optimizing a Trainium2 kernel written in Bass

```python
import numpy as np
import jax
import jax.numpy as jnp

def _softmax(x, axis=-1):
    return jax.nn.softmax(x, axis=axis)

def _gelu(x):
    return jax.nn.gelu(x, approximate=True)

def _silu(x):
    return jax.nn.silu(x)

def _sigmoid(x):
    return jax.nn.sigmoid(x)

def _layernorm(x, axis=-1, eps=1e-05):
    m = jnp.mean(x, axis=axis, keepdims=True)
    v = jnp.var(x, axis=axis, keepdims=True)
    return (x - m) / jnp.sqrt(v + eps)

def _scatter_add(tgt, idx, src, axis=0):
    return tgt.at[idx].add(src)

def _segment_sum(src, seg, n):
    return jax.ops.segment_sum(src, seg, n)
kernel_name = 'mk_rec_standalone_d1_rec_r8_047c03'

def setup_inputs(seed: int=0):
    np.random.seed(seed)
    _w = jnp.asarray

    def _rec_inputs():
        import jax
        import jax.numpy as jnp
        _rk = jax.random.key(seed)
        r_dense = -0.000171701 + 0.999137 * jax.random.normal(jax.random.fold_in(_rk, 1), (512, 13), jnp.float32)
        r_sparse = jnp.stack([jax.random.randint(jax.random.fold_in(jax.random.fold_in(_rk, 2), 0), (512,), 0, 9998, jnp.int32), jax.random.randint(jax.random.fold_in(jax.random.fold_in(_rk, 2), 1), (512,), 2, 1250, jnp.int32), jax.random.randint(jax.random.fold_in(jax.random.fold_in(_rk, 2), 2), (512,), 9, 9998, jnp.int32), jax.random.randint(jax.random.fold_in(jax.random.fold_in(_rk, 2), 3), (512,), 2, 9995, jnp.int32), jax.random.randint(jax.random.fold_in(jax.random.fold_in(_rk, 2), 4), (512,), 1, 9995, jnp.int32), jax.random.randint(jax.random.fold_in(jax.random.fold_in(_rk, 2), 5), (512,), 1, 1250, jnp.int32), jax.random.randint(jax.random.fold_in(jax.random.fold_in(_rk, 2), 6), (512,), 0, 9999, jnp.int32), jax.random.randint(jax.random.fold_in(jax.random.fold_in(_rk, 2), 7), (512,), 0, 1250, jnp.int32), jax.random.randint(jax.random.fold_in(jax.random.fold_in(_rk, 2), 8), (512,), 5, 9997, jnp.int32), jax.random.randint(jax.random.fold_in(jax.random.fold_in(_rk, 2), 9), (512,), 1, 9999, jnp.int32), jax.random.randint(jax.random.fold_in(jax.random.fold_in(_rk, 2), 10), (512,), 1, 9995, jnp.int32), jax.random.randint(jax.random.fold_in(jax.random.fold_in(_rk, 2), 11), (512,), 2, 9997, jnp.int32), jax.random.randint(jax.random.fold_in(jax.random.fold_in(_rk, 2), 12), (512,), 1, 9999, jnp.int32), jax.random.randint(jax.random.fold_in(jax.random.fold_in(_rk, 2), 13), (512,), 2, 9995, jnp.int32), jax.random.randint(jax.random.fold_in(jax.random.fold_in(_rk, 2), 14), (512,), 6, 1250, jnp.int32), jax.random.randint(jax.random.fold_in(jax.random.fold_in(_rk, 2), 15), (512,), 0, 1250, jnp.int32), jax.random.randint(jax.random.fold_in(jax.random.fold_in(_rk, 2), 16), (512,), 1, 9997, jnp.int32), jax.random.randint(jax.random.fold_in(jax.random.fold_in(_rk, 2), 17), (512,), 2, 9996, jnp.int32), jax.random.randint(jax.random.fold_in(jax.random.fold_in(_rk, 2), 18), (512,), 4, 1250, jnp.int32), jax.random.randint(jax.random.fold_in(jax.random.fold_in(_rk, 2), 19), (512,), 3, 9993, jnp.int32), jax.random.randint(jax.random.fold_in(jax.random.fold_in(_rk, 2), 20), (512,), 2, 9993, jnp.int32), jax.random.randint(jax.random.fold_in(jax.random.fold_in(_rk, 2), 21), (512,), 2, 1250, jnp.int32), jax.random.randint(jax.random.fold_in(jax.random.fold_in(_rk, 2), 22), (512,), 6, 1250, jnp.int32), jax.random.randint(jax.random.fold_in(jax.random.fold_in(_rk, 2), 23), (512,), 0, 9999, jnp.int32), jax.random.randint(jax.random.fold_in(jax.random.fold_in(_rk, 2), 24), (512,), 4, 9999, jnp.int32), jax.random.randint(jax.random.fold_in(jax.random.fold_in(_rk, 2), 25), (512,), 0, 9999, jnp.int32)], axis=1)
        return (r_dense, r_sparse)
    r_dense, r_sparse = _rec_inputs()

    def _L0_rec_setup():
        import jax, jax.numpy as jnp
        import numpy as np
        B, M, V, E, ND = (512, 26, 1250, 32, 13)
        CIN_LAYERS = (128, 128)
        DEEP = (1024, 512, 256)
        DEEP_IN = M * E + ND
        CIN_CORES = sum((h - h // 2 for h in CIN_LAYERS))

        def _xdeepfm(sparse, dense, tables, lin_sparse_w, lin_dense_w, conv1_w, conv1_b, conv2_w, conv2_b, cin_w, cin_b, W1, b1, W2, b2, W3, b3, deep_w, deep_b, bias):
            feat_idx = jnp.arange(M)
            emb = tables[feat_idx, sparse]
            linear_out = lin_sparse_w[feat_idx, sparse].sum(-1) + dense @ lin_dense_w
            x0 = emb
            xk = emb
            res = []
            for w, bb in ((conv1_w, conv1_b), (conv2_w, conv2_b)):
                h = xk.shape[1]
                hp = jnp.einsum('bhd,bmd->bhmd', xk, x0).reshape(-1, h * M, E)
                xn = jax.nn.sigmoid(jnp.einsum('oi,bid->bod', w, hp) + bb[None, :, None])
                half = xn.shape[1] // 2
                xk = xn[:, :half]
                res.append(xn[:, half:])
            cin_feat = jnp.concatenate(res, axis=1).sum(-1)
            cin_out = (cin_feat @ cin_w + cin_b)[:, 0]
            deep_x = jnp.concatenate([emb.reshape(-1, M * E), dense], axis=-1)
            h1 = jnp.tanh(deep_x @ W1 + b1)
            h2 = jnp.tanh(h1 @ W2 + b2)
            h3 = jnp.tanh(h2 @ W3 + b3)
            deep_out = (h3 @ deep_w + deep_b)[:, 0]
            return linear_out + cin_out + deep_out + bias[0]
        key = jax.random.key(seed)
        ks = jax.random.split(key, 20)

        def n(k, shp, s=0.05):
            return jax.random.normal(k, shp, dtype=jnp.float32) * s
        inp = {}
        inp['sparse'] = jax.random.randint(ks[0], (B, M), 0, V)
        inp['dense'] = jax.random.normal(ks[1], (B, ND), dtype=jnp.float32)
        inp['tables'] = n(ks[2], (M, V, E))
        inp['lin_sparse_w'] = n(ks[3], (M, V))
        inp['lin_dense_w'] = n(ks[4], (ND,))
        inp['conv1_w'] = n(ks[5], (CIN_LAYERS[0], M * M))
        inp['conv1_b'] = jnp.zeros((CIN_LAYERS[0],), jnp.float32)
        inp['conv2_w'] = n(ks[6], (CIN_LAYERS[1], CIN_LAYERS[0] // 2 * M))
        inp['conv2_b'] = jnp.zeros((CIN_LAYERS[1],), jnp.float32)
        inp['cin_w'] = n(ks[7], (CIN_CORES, 1))
        inp['cin_b'] = jnp.zeros((1,), jnp.float32)
        dims = [DEEP_IN] + list(DEEP)
        inp['W1'] = n(ks[8], (dims[0], dims[1]))
        inp['b1'] = jnp.zeros((dims[1],), jnp.float32)
        inp['W2'] = n(ks[9], (dims[1], dims[2]))
        inp['b2'] = jnp.zeros((dims[2],), jnp.float32)
        inp['W3'] = n(ks[10], (dims[2], dims[3]))
        inp['b3'] = jnp.zeros((dims[3],), jnp.float32)
        inp['deep_w'] = n(ks[11], (dims[3], 1))
        inp['deep_b'] = jnp.zeros((1,), jnp.float32)
        inp['bias'] = jnp.zeros((1,), jnp.float32)
        return inp
    _L0_rec_all = _L0_rec_setup()
    _L0_rec_in = {k: v for k, v in _L0_rec_all.items() if k in ('tables', 'lin_sparse_w', 'lin_dense_w', 'conv1_w', 'conv1_b', 'conv2_w', 'conv2_b', 'cin_w', 'cin_b', 'W1', 'b1', 'W2', 'b2', 'W3', 'b3', 'deep_w', 'deep_b', 'bias')}
    del _L0_rec_all
    return {'r_dense': r_dense, 'r_sparse': r_sparse, 'L0_rec_tables': _L0_rec_in['tables'], 'L0_rec_lin_sparse_w': _L0_rec_in['lin_sparse_w'], 'L0_rec_lin_dense_w': _L0_rec_in['lin_dense_w'], 'L0_rec_conv1_w': _L0_rec_in['conv1_w'], 'L0_rec_conv1_b': _L0_rec_in['conv1_b'], 'L0_rec_conv2_w': _L0_rec_in['conv2_w'], 'L0_rec_conv2_b': _L0_rec_in['conv2_b'], 'L0_rec_cin_w': _L0_rec_in['cin_w'], 'L0_rec_cin_b': _L0_rec_in['cin_b'], 'L0_rec_W1': _L0_rec_in['W1'], 'L0_rec_b1': _L0_rec_in['b1'], 'L0_rec_W2': _L0_rec_in['W2'], 'L0_rec_b2': _L0_rec_in['b2'], 'L0_rec_W3': _L0_rec_in['W3'], 'L0_rec_b3': _L0_rec_in['b3'], 'L0_rec_deep_w': _L0_rec_in['deep_w'], 'L0_rec_deep_b': _L0_rec_in['deep_b'], 'L0_rec_bias': _L0_rec_in['bias']}

def reference(r_dense, r_sparse, L0_rec_tables, L0_rec_lin_sparse_w, L0_rec_lin_dense_w, L0_rec_conv1_w, L0_rec_conv1_b, L0_rec_conv2_w, L0_rec_conv2_b, L0_rec_cin_w, L0_rec_cin_b, L0_rec_W1, L0_rec_b1, L0_rec_W2, L0_rec_b2, L0_rec_W3, L0_rec_b3, L0_rec_deep_w, L0_rec_deep_b, L0_rec_bias):
    import jax
    import jax.numpy as jnp

    def _L0_rec_ref(sparse, dense, tables, lin_sparse_w, lin_dense_w, conv1_w, conv1_b, conv2_w, conv2_b, cin_w, cin_b, W1, b1, W2, b2, W3, b3, deep_w, deep_b, bias):
        import jax, jax.numpy as jnp
        import numpy as np
        B, M, V, E, ND = (512, 26, 1250, 32, 13)
        CIN_LAYERS = (128, 128)
        DEEP = (1024, 512, 256)
        DEEP_IN = M * E + ND
        CIN_CORES = sum((h - h // 2 for h in CIN_LAYERS))

        def _xdeepfm(sparse, dense, tables, lin_sparse_w, lin_dense_w, conv1_w, conv1_b, conv2_w, conv2_b, cin_w, cin_b, W1, b1, W2, b2, W3, b3, deep_w, deep_b, bias):
            feat_idx = jnp.arange(M)
            emb = tables[feat_idx, sparse]
            linear_out = lin_sparse_w[feat_idx, sparse].sum(-1) + dense @ lin_dense_w
            x0 = emb
            xk = emb
            res = []
            for w, bb in ((conv1_w, conv1_b), (conv2_w, conv2_b)):
                h = xk.shape[1]
                hp = jnp.einsum('bhd,bmd->bhmd', xk, x0).reshape(-1, h * M, E)
                xn = jax.nn.sigmoid(jnp.einsum('oi,bid->bod', w, hp) + bb[None, :, None])
                half = xn.shape[1] // 2
                xk = xn[:, :half]
                res.append(xn[:, half:])
            cin_feat = jnp.concatenate(res, axis=1).sum(-1)
            cin_out = (cin_feat @ cin_w + cin_b)[:, 0]
            deep_x = jnp.concatenate([emb.reshape(-1, M * E), dense], axis=-1)
            h1 = jnp.tanh(deep_x @ W1 + b1)
            h2 = jnp.tanh(h1 @ W2 + b2)
            h3 = jnp.tanh(h2 @ W3 + b3)
            deep_out = (h3 @ deep_w + deep_b)[:, 0]
            return linear_out + cin_out + deep_out + bias[0]
        return _xdeepfm(sparse, dense, tables, lin_sparse_w, lin_dense_w, conv1_w, conv1_b, conv2_w, conv2_b, cin_w, cin_b, W1, b1, W2, b2, W3, b3, deep_w, deep_b, bias)
    y = _L0_rec_ref(r_sparse, r_dense, L0_rec_tables, L0_rec_lin_sparse_w, L0_rec_lin_dense_w, L0_rec_conv1_w, L0_rec_conv1_b, L0_rec_conv2_w, L0_rec_conv2_b, L0_rec_cin_w, L0_rec_cin_b, L0_rec_W1, L0_rec_b1, L0_rec_W2, L0_rec_b2, L0_rec_W3, L0_rec_b3, L0_rec_deep_w, L0_rec_deep_b, L0_rec_bias)
    return y

_drawn_inputs = setup_inputs


def setup_inputs(seed=0):
    import zlib

    import numpy as np

    out = dict(_drawn_inputs(seed))
    spreads = {'L0_rec_conv1_b': (0.0, 0.408),
     'L0_rec_conv2_b': (0.0, 0.344),
     'L0_rec_b1': (0.0, 0.8),
     'L0_rec_b2': (0.0, 0.8),
     'L0_rec_b3': (0.0, 0.8)}
    factors = {'r_dense': 3.456,
     'L0_rec_tables': 8.0,
     'L0_rec_lin_sparse_w': 4.15,
     'L0_rec_lin_dense_w': 4.201,
     'L0_rec_conv1_w': 8.0,
     'L0_rec_conv2_w': 8.0,
     'L0_rec_W1': 2.767,
     'L0_rec_W3': 3.716,
     'L0_rec_deep_w': 2.828}
    for name, (base, spread) in spreads.items():
        noise = np.random.default_rng([zlib.crc32(name.encode()), seed]).standard_normal(out[name].shape)
        drawn = base * np.exp(spread * noise) if base else spread * noise
        out[name] = jnp.asarray(drawn.astype(out[name].dtype))
    for name, factor in factors.items():
        out[name] = (out[name] * factor).astype(out[name].dtype)
    return out
```

```python
from contextlib import ExitStack

import concourse.bass as bass
from concourse import mybir

F32 = mybir.dt.float32
F32R = mybir.dt.float32r
BF16 = mybir.dt.bfloat16
I32 = mybir.dt.int32
U32 = mybir.dt.uint32
ALU = mybir.AluOpType
ACT = mybir.ActivationFunctionType
AX = mybir.AxisListType

P = 128
B, M, V, E, ND = 512, 26, 1250, 32, 13
BT = B // P
ROW = E + 1
HALF = 64
CH = 512
NPAIR = B * E // (2 * CH)
GP = NPAIR // BT
DP = E // GP
NPR = M * (M + 1) // 2
UT = 3
UK = NPR // UT
T2 = M * HALF // P
XR = 3 * M
D1, D2, D3 = 1024, 512, 256
K1 = 7
K1_LAST = M * E + ND - (K1 - 1) * P
EMB_LAST = M * E - (K1 - 1) * P
K2, K3 = D1 // P, D2 // P
WP = 1024
C_B1, C_B2, C_B3, C_DEEP, C_CB1, C_CB2, C_CIN1, C_CIN2, C_AUX, C_END = 0, 8, 12, 14, 16, 17, 18, 19, 20, 21



def build(nc, idx, idx_base, table, dense_t, w1a, w1b, w1_fix, w2, mlp1, mlp2, mlp3, small, sel1, sel2,
          ident, ident_bf, out):
    with ExitStack() as ctx:
        def sb(name, shape, dt=F32):
            return ctx.enter_context(nc.sbuf_tensor(name, shape, dt))

        def ps(name, shape, dt=F32):
            return ctx.enter_context(nc.psum_tensor(name, shape, dt))

        def sem(name):
            return ctx.enter_context(nc.semaphore(name))

        small_sb = sb("small_sb", [P, C_END])
        sel1_sb = sb("sel1_sb", [XR, UT, UK], BF16)
        sel2_sb = sb("sel2_sb", [XR, T2, P], BF16)
        ident_sb = sb("ident_sb", [P, P])
        identb_sb = sb("identb_sb", [P, P], BF16)
        w1_hi = sb("w1_hi", [UK, UT, P], F32R)
        w1_lo = sb("w1_lo", [UK, UT, P], F32R)
        w2_sb = sb("w2_sb", [P, T2, HALF])
        m1_hi = sb("m1_hi", [P, K1, D1], F32R)
        m1_lo = sb("m1_lo", [P, K1, D1], F32R)
        m2_hi = sb("m2_hi", [P, K2, D2], F32R)
        m2_lo = sb("m2_lo", [P, K2, D2], F32R)
        m3_hi = sb("m3_hi", [P, K3, D3], F32R)
        m3_lo = sb("m3_lo", [P, K3, D3], F32R)
        rows = sb("rows", [P, BT, M], U32)
        emb = sb("emb", [P, BT, M, ROW])
        res1 = [sb(f"res1_{k}", [P, CH]) for k in range(2)]
        res2 = [sb(f"res2_{k}", [P, CH]) for k in range(2)]
        with ExitStack() as sums_of_d:
            acc1 = sums_of_d.enter_context(nc.sbuf_tensor("acc1", [P, BT, CH], F32))
            acc2 = sums_of_d.enter_context(nc.sbuf_tensor("acc2", [P, BT + 1, CH], F32))
        h1_lo = sb("h1_lo", [P, 2 * BT + 1, CH], F32R)[:, 0:K2, :]
        aux = sb("aux", [P, B])
        lin = sb("lin", [P, BT])
        with ExitStack() as early:
            idx_sb = early.enter_context(nc.sbuf_tensor("idx_sb", [P, BT, M], I32))
            base_sb = early.enter_context(nc.sbuf_tensor("base_sb", [P, BT, M], I32))
            wrap = early.enter_context(nc.sbuf_tensor("wrap", [P, BT, M], F32))
            inside = early.enter_context(nc.sbuf_tensor("inside", [P, BT, M], F32))
            clamped = early.enter_context(nc.sbuf_tensor("clamped", [P, BT, M], F32))
            w1a_sb = early.enter_context(nc.sbuf_tensor("w1a_sb", [UK, UT, P], F32))
            w1b_sb = early.enter_context(nc.sbuf_tensor("w1b_sb", [UK, UT, P], F32))
            fix_sb = early.enter_context(nc.sbuf_tensor("fix_sb", [UK, UT, M], F32))
        prod = [sb(f"prod{k}", [P, 2, CH]) for k in range(2)]
        with ExitStack() as cin:
            rest = cin.enter_context(nc.sbuf_tensor("rest", [P, M, E], F32))
            parts = cin.enter_context(nc.sbuf_tensor("parts", [P, E, 3, M], BF16))
            sq = cin.enter_context(nc.sbuf_tensor("sq", [UK, UT, CH], F32))
            sq_hi = cin.enter_context(nc.sbuf_tensor("sq_hi", [UK, UT, CH], F32R))
            sq_lo = cin.enter_context(nc.sbuf_tensor("sq_lo", [UK, UT, CH], F32R))
            x = [cin.enter_context(nc.sbuf_tensor(f"x{k}", [XR, 2 * CH], BF16)) for k in range(2)]
            xk = [cin.enter_context(nc.sbuf_tensor(f"xk{k}", [P, 2, CH], F32)) for k in range(2)]
            wpiece = [cin.enter_context(nc.sbuf_tensor(f"wpiece{k}", [P, WP], F32)) for k in range(2)]
        xt_hi = sb("xt_hi", [P, K1, B], F32R)
        xt_lo = sb("xt_lo", [P, K1, B], F32R)
        h1_hi = sb("h1_hi", [P, K2, B], F32R)
        packed = [w[:, 0:B].rearrange("p (t n) -> p t n", t=BT) for w in wpiece]
        h2_hi, h2_lo = xt_hi, xt_lo
        hf = [prod[0][:, k, :] for k in range(2)]
        h3 = prod[1]
        fold1 = res1[0][:, :].rearrange("p (t b) -> p t b", t=BT)
        fold2 = res1[1][:, :].rearrange("p (t b) -> p t b", t=BT)
        row_sb = res2[0][0:1, :]

        spread = [ps(f"spread{k}", [P, 2, CH]) for k in range(2)]
        l2out = [ps(f"l2out{k}", [P, CH]) for k in range(2)]
        l1out = ps("l1out", [P, CH])
        stage = ps("stage", [P, CH])
        stage_bf = stage[:, :].bitcast(BF16)
        row_ps = l2out[0]

        idx_in, base_in, small_in = sem("idx_in"), sem("base_in"), sem("small_in")
        w1_in, w2_in, sel_in, ident_in, dense_in = (sem("w1_in"), sem("w2_in"), sem("sel_in"),
                                                    sem("ident_in"), sem("dense_in"))
        piece_in = [sem("piece_in0"), sem("piece_in1")]
        piece_hi, piece_lo = sem("piece_hi"), sem("piece_lo")
        idx_step = sem("idx_step")
        emb_in = sem("emb_in")
        zeroed = sem("zeroed")
        w1_step = sem("w1_step")
        fix_done = sem("fix_done")
        split_step = sem("split_step")
        turned = sem("turned")
        x_ready = sem("x_ready")
        sums_done = sem("sums_done")
        hi_done = sem("hi_done")
        lo_done = sem("lo_done")
        l1_done = sem("l1_done")
        l1_read = sem("l1_read")
        xk_ready = sem("xk_ready")
        spread_done = sem("spread_done")
        prod_done = sem("prod_done")
        main_done = sem("main_done")
        res2_ready = sem("res2_ready")
        add1_done, add2_done = sem("add1_done"), sem("add2_done")
        pack_done = sem("pack_done")
        xt_done, xt_hi_done, xt_lo_done = sem("xt_done"), sem("xt_hi_done"), sem("xt_lo_done")
        dense_split = sem("dense_split")
        mlp_done = sem("mlp_done")
        tanh_done, h_hi_done, h_lo_done = sem("tanh_done"), sem("h_hi_done"), sem("h_lo_done")
        fold_step = sem("fold_step")
        row_done, row_read, out_done = sem("row_done"), sem("row_read"), sem("out_done")

        NTILE = NPAIR * T2
        PIECES = K1 + K2 // 2 + 1
        ROWS_IN = 16 * M
        MLP_BANKS = [l1out, stage]
        MT = [D1 // P, D2 // P, D3 // P]
        HT = sum(MT)

        def slot(g, t):
            return g * T2 + t

        block = ctx.enter_context(nc.Block())

        @block.sync
        def _(sp):
            sp.dma_start(idx_sb[:, :, :], idx.rearrange("(t p) m -> p t m", p=P)).then_inc(idx_in, 16)
            sp.dma_start(base_sb[:, :, :], idx_base).then_inc(base_in, 16)
            sp.dma_start(w1a_sb[:, :, :], w1a).then_inc(w1_in, 16)
            sp.dma_start(w1b_sb[:, :, :], w1b).then_inc(w1_in, 16)
            sp.dma_start(fix_sb[:, :, :], w1_fix).then_inc(w1_in, 16)
            sp.dma_start(identb_sb[:, :], ident_bf).then_inc(ident_in, 16)
            sp.dma_start(ident_sb[:, :], ident).then_inc(ident_in, 16)
            sp.dma_start(sel1_sb[:, :, :], sel1).then_inc(sel_in, 16)
            sp.dma_start(sel2_sb[:, :, :], sel2).then_inc(sel_in, 16)
            sp.dma_start(small_sb[:, :], small).then_inc(small_in, 16)
            sp.dma_start(w2_sb[:, :, :], w2).then_inc(w2_in, 16)
            sp.wait_ge(zeroed, 1)
            sp.dma_start(aux[EMB_LAST:EMB_LAST + ND, :], dense_t).then_inc(dense_in, 16)
            for k in range(PIECES):
                if k >= 2:
                    sp.wait_ge(piece_lo, k - 1)
                if k < K1:
                    n = P if k < K1 - 1 else K1_LAST
                    dst, src = wpiece[k % 2][0:n, :], mlp1[k * P:k * P + n, :]
                elif k < PIECES - 1:
                    j = 2 * (k - K1)
                    dst = wpiece[k % 2][:, :].rearrange("p (k n) -> p k n", k=2)
                    src = mlp2[j * P:(j + 2) * P, :].rearrange("(k p) n -> p k n", p=P)
                else:
                    dst = wpiece[k % 2][:, :].rearrange("p (k n) -> p k n", k=K3)
                    src = mlp3.rearrange("(k p) n -> p k n", p=P)
                sp.dma_start(dst, src).then_inc(piece_in[k % 2], 16)
            sp.wait_ge(row_read, 1)
            sp.dma_start(out.rearrange("(a b) -> a b", a=1), row_sb).then_inc(out_done, 16)
            sp.wait_ge(out_done, 16)

        @block.gpsimd
        def _(pool):
            pool.wait_ge(idx_step, 5)
            for b in range(BT):
                for m in range(M):
                    pool.indirect_dma_start(
                        out=emb[:, b, m, :], out_offset=None, in_=table,
                        in_offset=bass.IndirectOffsetOnAxis(ap=rows[:, b, m:m + 1], axis=0),
                    ).then_inc(emb_in, 16)
                pool.wait_ge(emb_in, ROWS_IN * (b + 1))
            for k in range(PIECES):
                n = K1_LAST if k == K1 - 1 else P
                if k < K1:
                    hi, lo = m1_hi[0:n, k, :], m1_lo[0:n, k, :]
                elif k < PIECES - 1:
                    j = 2 * (k - K1)
                    hi = m2_hi[:, j:j + 2, :].rearrange("p k n -> p (k n)")
                    lo = m2_lo[:, j:j + 2, :].rearrange("p k n -> p (k n)")
                else:
                    hi = m3_hi[:, :, :].rearrange("p k n -> p (k n)")
                    lo = m3_lo[:, :, :].rearrange("p k n -> p (k n)")
                pool.wait_ge(piece_in[k % 2], 16 * (k // 2 + 1))
                nc.gpsimd.tensor_copy(hi, wpiece[k % 2][0:n, :]).then_inc(piece_hi, 1)
                pool.wait_ge(piece_hi, k + 1)
                nc.gpsimd.tensor_tensor(lo, wpiece[k % 2][0:n, :], hi.bitcast(F32),
                                        ALU.subtract).then_inc(piece_lo, 1)

            pool.wait_ge(piece_lo, PIECES)
            for k in range(K1):
                n = (P if k < K1 - 1 else EMB_LAST) // E
                if k >= 2:
                    pool.wait_ge(xt_done, k - 1)
                nc.gpsimd.tensor_copy(packed[k % 2][:, :, 0:n * E].rearrange("p t (m d) -> p t m d", d=E),
                                      emb[:, :, 4 * k:4 * k + n, 0:E]).then_inc(pack_done, 1)

        @block.tensor
        def _(pe):
            def turn(g):
                for d in range(DP):
                    mm = nc.tensor.transpose(stage_bf[0:XR, d * P:(d + 1) * P],
                                             parts[:, g * DP + d, :, :].rearrange("p a m -> p (a m)"),
                                             identb_sb[:, :])
                mm.then_inc(turned, 1)

            def sums(c, u, chunk, xp):
                if c + u > 0:
                    pe.wait_ge(hi_done, UT * chunk + u)
                nc.tensor.matmul(stage[0:UK, :], sel1_sb[:, u, :], xp[:, c * CH:(c + 1) * CH],
                                 start=True, stop=True).then_inc(sums_done, 1)

            def layer1(chunk):
                pe.wait_ge(lo_done, chunk + 1)
                if not (isinstance(chunk, int) and chunk == 0):
                    pe.wait_ge(l1_read, chunk)
                k = 0
                for u in range(UT):
                    for w, s in ((w1_hi, sq_hi), (w1_lo, sq_hi), (w1_hi, sq_lo)):
                        mm = nc.tensor.matmul(l1out[:, :], w[:, u, :], s[:, u, :],
                                              start=(k == 0), stop=(k == 3 * UT - 1))
                        k += 1
                mm.then_inc(l1_done, 1)

            def spread_tile(t, k, xp):
                for c in range(2):
                    mm = nc.tensor.matmul(spread[k % 2][:, c, :], sel2_sb[:, t, :],
                                          xp[:, c * CH:(c + 1) * CH], start=True, stop=True)
                mm.then_inc(spread_done, 1)

            def main(t, k, lo):
                for c in range(2):
                    mm = nc.tensor.matmul(lo[c * HALF:(c + 1) * HALF, :], w2_sb[:, t, :],
                                          prod[k % 2][:, c, :], start=(t == 0), stop=(t == T2 - 1))
                mm.then_inc(main_done, 1)

            def turn_embeddings(k):
                if k:
                    pe.wait_ge(xt_lo_done, k)
                pe.wait_ge(pack_done, k + 1)
                n = P if k < K1 - 1 else EMB_LAST
                for b in range(BT):
                    mm = nc.tensor.transpose(stage[0:n, b * P:(b + 1) * P],
                                             packed[k % 2][:, b, 0:n], ident_sb[:, :])
                mm.then_inc(xt_done, 1)

            def pairs(b, last):
                for g in range(GP):
                    i = b * GP + g
                    end = last and g == GP - 1
                    nxt = x[(g + 1) % 2]
                    for t in range(T2):
                        k = slot(g, t)
                        pe.wait_ge(prod_done, i * T2 + t + 1)
                        main(t, k, l2out[g % 2])
                        if t + 2 < T2:
                            spread_tile(t + 2, k + 2, x[g % 2])
                        elif not end:
                            spread_tile(t + 2 - T2, k + 2, nxt)
                        if end:
                            if t % 2 == 0:
                                if t == 0:
                                    pe.wait_ge(hi_done, UT * 2 * NPAIR)
                                turn_embeddings(t // 2)
                            continue
                        if t == 0:
                            pe.wait_ge(x_ready, i + 2)
                        if t < 3:
                            sums(0, t, 2 * i + 2, nxt)
                        if t == 4:
                            layer1(2 * i + 2)
                        if 5 <= t < 8:
                            sums(1, t - 5, 2 * i + 3, nxt)
                        if t == 9:
                            layer1(2 * i + 3)
                        if t == 10 and not (last and g >= 2):
                            pe.wait_ge(split_step, 4 * (b + (1 if g < 2 else 2)))
                            pe.wait_ge(hi_done, UT * (2 * i + 4))
                            turn((g + 2) % 4)

            pe.wait_ge(w1_in, 48)
            pe.wait_ge(w1_step, 2)
            for u in range(UT):
                mm = nc.tensor.matmul(l1out[0:M, 0:P], fix_sb[:, u, :], w1a_sb[:, u, :],
                                      start=(u == 0), stop=(u == UT - 1))
            mm.then_inc(fix_done, 1)
            pe.wait_ge(ident_in, 32)
            pe.wait_ge(split_step, 4)
            turn(0)
            pe.wait_ge(x_ready, 1)
            turn(1)
            pe.wait_ge(sel_in, 32)
            pe.wait_ge(x_ready, 2)
            for c in range(2):
                for u in range(UT):
                    sums(c, u, c, x[0])
                if c == 0:
                    pe.wait_ge(w1_step, 5)
                layer1(c)
            pe.wait_ge(w2_in, 16)
            spread_tile(0, 0, x[0])
            spread_tile(1, 1, x[0])

            with pe.Fori(0, BT - 1) as b:
                pairs(b, False)
            pairs(BT - 1, True)

            pe.wait_ge(piece_lo, PIECES)
            pe.wait_ge(dense_split, 2)
            pe.wait_ge(xt_lo_done, K1)
            pe.wait_ge(l1_read, 2 * NPAIR)
            n = 0
            for layer, (hi, lo, kt, xh, xl) in enumerate((
                    (m1_hi, m1_lo, K1, xt_hi, xt_lo), (m2_hi, m2_lo, K2, h1_hi, h1_lo),
                    (m3_hi, m3_lo, K3, h2_hi, h2_lo))):
                before = sum(MT[:layer])
                for mt in range(MT[layer]):
                    if n >= 2:
                        pe.wait_ge(tanh_done, n - 1)
                    for k in range(kt):
                        if layer and mt == 0:
                            pe.wait_ge(h_lo_done, before - kt + k + 1)
                        r = K1_LAST if layer == 0 and k == K1 - 1 else P
                        for j, (w, h) in enumerate(((hi, xh), (lo, xh), (hi, xl))):
                            mm = nc.tensor.matmul(MLP_BANKS[n % 2][:, :], w[0:r, k, mt * P:(mt + 1) * P],
                                                  h[0:r, k, :], start=(k == 0 and j == 0),
                                                  stop=(k == kt - 1 and j == 2))
                    mm.then_inc(mlp_done, 1)
                    n += 1
                if layer == 0:
                    pe.wait_ge(fold_step, 6)
                    pe.wait_ge(small_in, 16)
                    pe.wait_ge(dense_in, 16)
                    pe.wait_ge(res2_ready, NPAIR + 1)
                    row = row_ps[0:1, :]
                    nc.tensor.matmul(row, small_sb[:, C_AUX:C_AUX + 1], aux[:, :], start=True, stop=False)
                    for c, f in ((C_CIN1, fold1), (C_CIN2, fold2)):
                        nc.tensor.matmul(row, small_sb[:, c:c + 1], f[:, :, :].rearrange("p t b -> p (t b)"),
                                         start=False, stop=False)
                    for t in range(BT):
                        nc.tensor.matmul(row_ps[0:1, t * P:(t + 1) * P], lin[:, t:t + 1], ident_sb[:, :],
                                         start=False, stop=False, skip_group_check=True)
            for k in range(D3 // P):
                pe.wait_ge(tanh_done, HT - D3 // P + k + 1)
                mm = nc.tensor.matmul(row_ps[0:1, :], small_sb[:, C_DEEP + k:C_DEEP + k + 1], h3[:, k, :],
                                      start=False, stop=(k == D3 // P - 1))
            mm.then_inc(row_done, 1)

        @block.scalar
        def _(act):
            def copy_x(pair, k):
                act.wait_ge(turned, pair + 1)
                nc.scalar.activation(x[k][:, :], stage_bf[0:XR, :], ACT.Copy).then_inc(x_ready, 1)

            def squares(chunk):
                if not (isinstance(chunk, int) and chunk == 0):
                    act.wait_ge(lo_done, chunk)
                    act.wait_ge(l1_done, chunk)
                for u in range(UT):
                    act.wait_ge(sums_done, chunk * UT + u + 1)
                    nc.scalar.activation(sq[:, u, :], stage[0:UK, :], ACT.Square)
                    nc.scalar.activation(sq_hi[:, u, :], stage[0:UK, :], ACT.Square).then_inc(hi_done, 1)

            def sigmoids(c, chunk, k):
                act.wait_ge(l1_done, chunk + 1)
                for q in range(2):
                    nc.scalar.activation(xk[k][q * HALF:(q + 1) * HALF, c, :], l1out[0:HALF, :], ACT.Sigmoid,
                                         bias=small_sb[0:HALF, C_CB1:C_CB1 + 1]).then_inc(xk_ready, 1)
                nc.scalar.activation(res1[k][c * HALF:(c + 1) * HALF, :], l1out[HALF:P, :], ACT.Sigmoid,
                                     bias=small_sb[HALF:P, C_CB1:C_CB1 + 1]).then_inc(l1_read, 1)

            def pairs(b, last):
                for g in range(GP):
                    i = b * GP + g
                    end = last and g == GP - 1
                    if not end:
                        for c in range(2):
                            squares(2 * i + 2 + c)
                            if c == 0:
                                act.wait_ge(prod_done, i * T2 + 1)
                            sigmoids(c, 2 * i + 2 + c, (g + 1) % 2)
                        if not (last and g >= 2):
                            copy_x(i + 2, g % 2)
                    else:
                        for k in range(K1):
                            n = P if k < K1 - 1 else EMB_LAST
                            if k == 0:
                                act.wait_ge(dense_in, 16)
                                nc.scalar.activation(xt_hi[EMB_LAST:EMB_LAST + ND, K1 - 1, :],
                                                     aux[EMB_LAST:EMB_LAST + ND, :],
                                                     ACT.Copy).then_inc(dense_split, 1)
                            act.wait_ge(xt_done, k + 1)
                            nc.scalar.activation(xt_hi[0:n, k, :], stage[0:n, :], ACT.Copy)\
                              .then_inc(xt_hi_done, 1)
                    act.wait_ge(main_done, (i + 1) * T2)
                    nc.scalar.activation(res2[g % 2][:, :], l2out[g % 2][:, :], ACT.Sigmoid,
                                         bias=small_sb[:, C_CB2:C_CB2 + 1]).then_inc(res2_ready, 1)

            for k in range(2):
                copy_x(k, k)
            act.wait_ge(small_in, 16)
            for c in range(2):
                squares(c)
                sigmoids(c, c, 0)

            with act.Fori(0, BT - 1) as b:
                pairs(b, False)
            pairs(BT - 1, True)

            n = 0
            for layer, bias in enumerate((C_B1, C_B2, C_B3)):
                for mt in range(MT[layer]):
                    act.wait_ge(mlp_done, n + 1)
                    if layer < 2 and n >= 2:
                        act.wait_ge(h_lo_done, n - 1)
                    dst = hf[n % 2] if layer < 2 else h3[:, mt, :]
                    nc.scalar.activation(dst, MLP_BANKS[n % 2][:, :], ACT.Tanh,
                                         bias=small_sb[:, bias + mt:bias + mt + 1]).then_inc(tanh_done, 1)
                    n += 1

        @block.vector
        def _(dve):
            def split(b, step):
                e = emb[:, bass.ds(b, 1), :, 0:E].rearrange("p t m d -> p (t m) d") if not isinstance(b, int) \
                    else emb[:, b, :, 0:E]
                part = [parts[:, :, j, :].rearrange("p d m -> p m d") for j in range(3)]
                if step == 0:
                    ins = nc.vector.tensor_copy(part[0], e)
                elif step == 1:
                    ins = nc.vector.tensor_tensor(rest[:, :, :], e, part[0], ALU.subtract)
                elif step == 2:
                    ins = nc.vector.tensor_copy(part[1], rest[:, :, :])
                else:
                    ins = nc.vector.tensor_tensor(part[2], rest[:, :, :], part[1], ALU.subtract)
                ins.then_inc(split_step, 1)

            def low(chunk):
                if not (isinstance(chunk, int) and chunk == 0):
                    dve.wait_ge(l1_done, chunk)
                dve.wait_ge(hi_done, UT * (chunk + 1))
                nc.vector.tensor_tensor(sq_lo[:, :, :].rearrange("p u n -> p (u n)"),
                                        sq[:, :, :].rearrange("p u n -> p (u n)"),
                                        sq_hi[:, :, :].rearrange("p u n -> p (u n)").bitcast(F32),
                                        ALU.subtract).then_inc(lo_done, 1)

            def block_of(a, b, off):
                if isinstance(b, int):
                    return a[:, b + off, :]
                return a[:, bass.ds(b + off, 1), :].rearrange("p t n -> p (t n)")

            def pairs(b, last):
                for g in range(GP):
                    i = b * GP + g
                    end = last and g == GP - 1
                    for t in range(T2):
                        k = slot(g, t)
                        dve.wait_ge(spread_done, i * T2 + t + 1)
                        if t == 0:
                            dve.wait_ge(xk_ready, 4 * (i + 1))
                        nc.vector.tensor_tensor(prod[k % 2][:, :, :].rearrange("p c n -> p (c n)"),
                                                spread[k % 2][:, :, :].rearrange("p c n -> p (c n)"),
                                                xk[g % 2][:, :, :].rearrange("p c n -> p (c n)"),
                                                ALU.mult).then_inc(prod_done, 1)
                        if t == 3 and not end:
                            low(2 * i + 2)
                        if t == 8 and not end:
                            low(2 * i + 3)
                        if t == 10:
                            dve.wait_ge(l1_read, 2 * (i + 1))
                            a = block_of(acc1, b, 0)
                            nc.vector.tensor_tensor(a, a, res1[g % 2][:, :], ALU.add).then_inc(add1_done, 1)
                        if t == 5:
                            dve.wait_ge(res2_ready, i + 1)
                            a = block_of(acc2, b, 0 if g == 0 else 1)
                            nc.vector.tensor_tensor(a, a, res2[(g + 1) % 2][:, :], ALU.add)\
                              .then_inc(add2_done, 1)
                        if g == 2 and not last and t in (0, 2, 4, 6):
                            if t == 0:
                                dve.wait_ge(emb_in, ROWS_IN * (b + 2))
                                dve.wait_ge(turned, 4 * (b + 1))
                            else:
                                dve.wait_ge(split_step, 4 * (b + 1) + t // 2)
                            split(b + 1, t // 2)
                        if end and t % 2 == 0:
                            tile = t // 2
                            n = P if tile < K1 - 1 else EMB_LAST
                            dve.wait_ge(xt_hi_done, tile + 1)
                            nc.vector.tensor_tensor(xt_lo[0:n, tile, :], stage[0:n, :],
                                                    xt_hi[0:n, tile, :].bitcast(F32), ALU.subtract)\
                              .then_inc(xt_lo_done, 1)

            dve.wait_ge(idx_in, 16)
            nc.vector.tensor_scalar(wrap[:, :, :], idx_sb[:, :, :], 0.0, float(V), ALU.is_lt, ALU.mult)\
              .then_inc(idx_step, 1)
            dve.wait_ge(idx_step, 1)
            nc.vector.tensor_tensor(inside[:, :, :], idx_sb[:, :, :], wrap[:, :, :], ALU.add).then_inc(idx_step, 1)
            dve.wait_ge(idx_step, 2)
            nc.vector.tensor_scalar(clamped[:, :, :], inside[:, :, :], 0.0, float(V - 1), ALU.max, ALU.min)\
              .then_inc(idx_step, 1)
            dve.wait_ge(base_in, 16)
            dve.wait_ge(idx_step, 3)
            nc.vector.tensor_tensor(rows[:, :, :], clamped[:, :, :], base_sb[:, :, :], ALU.add).then_inc(idx_step, 2)
            nc.vector.memset(aux[:, :], 1.0).then_inc(zeroed, 1)
            nc.vector.memset(acc1[:, :, :], 0.0).then_inc(zeroed, 1)
            nc.vector.memset(acc2[:, :, :], 0.0).then_inc(zeroed, 1)
            nc.vector.memset(res2[1][:, :], 0.0).then_inc(res2_ready, 1)
            dve.wait_ge(w1_in, 48)
            nc.vector.tensor_tensor(w1b_sb[:, :, :], w1a_sb[:, :, :], w1b_sb[:, :, :], ALU.add).then_inc(w1_step, 1)
            dve.wait_ge(w1_step, 1)
            nc.vector.tensor_scalar(w1a_sb[:, :, :], w1b_sb[:, :, :], 0.5, None, ALU.mult).then_inc(w1_step, 1)
            dve.wait_ge(fix_done, 1)
            nc.vector.tensor_copy(w1a_sb[0:M, 0, :], l1out[0:M, 0:P]).then_inc(w1_step, 1)
            dve.wait_ge(w1_step, 3)
            nc.vector.tensor_copy(w1_hi[:, :, :], w1a_sb[:, :, :]).then_inc(w1_step, 1)
            dve.wait_ge(w1_step, 4)
            nc.vector.tensor_tensor(w1_lo[:, :, :], w1a_sb[:, :, :], w1_hi[:, :, :].bitcast(F32),
                                    ALU.subtract).then_inc(w1_step, 1)
            dve.wait_ge(zeroed, 3)
            dve.wait_ge(emb_in, ROWS_IN)
            for step in range(4):
                if step:
                    dve.wait_ge(split_step, step)
                split(0, step)
            for c in range(2):
                low(c)

            with dve.Fori(0, BT - 1) as b:
                pairs(b, False)
            pairs(BT - 1, True)

            dve.wait_ge(dense_split, 1)
            nc.vector.tensor_tensor(xt_lo[EMB_LAST:EMB_LAST + ND, K1 - 1, :], aux[EMB_LAST:EMB_LAST + ND, :],
                                    xt_hi[EMB_LAST:EMB_LAST + ND, K1 - 1, :].bitcast(F32), ALU.subtract)\
              .then_inc(dense_split, 1)
            nc.vector.tensor_reduce(lin[:, :], emb[:, :, :, E], AX.X, ALU.add).then_inc(fold_step, 1)
            dve.wait_ge(res2_ready, NPAIR + 1)
            nc.vector.tensor_tensor(acc2[:, BT, :], acc2[:, BT, :], res2[1][:, :], ALU.add).then_inc(fold_step, 1)
            dve.wait_ge(add1_done, NPAIR)
            dve.wait_ge(fold_step, 2)
            for a, f, n in ((acc1[:, :, :], fold1, 3), (acc2[:, 1:BT + 1, :], fold2, 5)):
                half = a[:, :, 0:2 * P]
                nc.vector.tensor_tensor(half, half, a[:, :, 2 * P:4 * P], ALU.add).then_inc(fold_step, 1)
                dve.wait_ge(fold_step, n)
                nc.vector.tensor_tensor(f[:, :, :], a[:, :, 0:P], a[:, :, P:2 * P], ALU.add)\
                  .then_inc(fold_step, 1)

            n = 0
            for layer, (hi, lo) in enumerate(((h1_hi, h1_lo), (h2_hi, h2_lo))):
                for mt in range(MT[layer]):
                    dve.wait_ge(tanh_done, n + 1)
                    if layer and mt == 0:
                        dve.wait_ge(mlp_done, MT[0])
                    nc.vector.tensor_copy(hi[:, mt, :], hf[n % 2]).then_inc(h_hi_done, 1)
                    dve.wait_ge(h_hi_done, n + 1)
                    nc.vector.tensor_tensor(lo[:, mt, :], hf[n % 2], hi[:, mt, :].bitcast(F32),
                                            ALU.subtract).then_inc(h_lo_done, 1)
                    n += 1
            dve.wait_ge(row_done, 1)
            nc.vector.tensor_copy(row_sb, row_ps[0:1, :]).then_inc(row_read, 1)


def kernel(r_dense, r_sparse, L0_rec_tables, L0_rec_lin_sparse_w, L0_rec_lin_dense_w, L0_rec_conv1_w,
           L0_rec_conv1_b, L0_rec_conv2_w, L0_rec_conv2_b, L0_rec_cin_w, L0_rec_cin_b, L0_rec_W1, L0_rec_b1,
           L0_rec_W2, L0_rec_b2, L0_rec_W3, L0_rec_b3, L0_rec_deep_w, L0_rec_deep_b, L0_rec_bias):
    import ml_dtypes
    import numpy as np
    import concourse.bacc as bacc
    from concourse.bass_utils import run_bass_kernel_spmd

    a = np.asarray
    f32, bf = np.float32, ml_dtypes.bfloat16
    first = np.array([m for m in range(M)] + [m for m in range(M) for n in range(m + 1, M)])
    second = np.array([m for m in range(M)] + [n for m in range(M) for n in range(m + 1, M)])
    tiles = lambda w: np.ascontiguousarray(w.reshape(UT, UK, -1).transpose(1, 0, 2))
    conv1 = a(L0_rec_conv1_w).reshape(P, M, M)
    conv2 = a(L0_rec_conv2_w)[HALF:].reshape(HALF, HALF, T2, 2)
    pair_of = np.arange(NPR)
    sel1 = np.zeros((3, M, NPR), bf)
    sel1[:, first, pair_of] = 1
    sel1[:, second, pair_of] = 1
    sel2 = np.zeros((3, M, T2, 2, HALF), bf)
    fix = np.zeros((NPR, M), f32)
    fix[pair_of, first] = -1
    fix[pair_of, second] = -1
    fix[np.arange(M), np.arange(M)] = 1
    for t in range(T2):
        for j in range(2):
            sel2[:, 2 * t + j, t, j, :] = 1
    small = np.zeros((P, C_END), f32)
    small[:, C_B1:C_B2] = a(L0_rec_b1).reshape(-1, P).T
    small[:, C_B2:C_B3] = a(L0_rec_b2).reshape(-1, P).T
    small[:, C_B3:C_DEEP] = a(L0_rec_b3).reshape(-1, P).T
    small[:, C_DEEP:C_CB1] = a(L0_rec_deep_w).reshape(-1, P).T
    small[:, C_CB1] = a(L0_rec_conv1_b)
    for j in range(2):
        small[j * HALF:(j + 1) * HALF, C_CB2] = a(L0_rec_conv2_b)[HALF:]
        small[j * HALF:(j + 1) * HALF, C_CIN1] = a(L0_rec_cin_w)[:HALF, 0]
        small[j * HALF:(j + 1) * HALF, C_CIN2] = a(L0_rec_cin_w)[HALF:, 0]
    small[0, C_AUX], small[1, C_AUX], small[2, C_AUX] = a(L0_rec_cin_b)[0], a(L0_rec_deep_b)[0], a(L0_rec_bias)[0]
    small[EMB_LAST:EMB_LAST + ND, C_AUX] = a(L0_rec_lin_dense_w)

    arrays = {
        "idx": a(r_sparse),
        "idx_base": np.ascontiguousarray(np.broadcast_to(np.arange(M, dtype=np.int32) * V, (P, BT, M))),
        "table": np.concatenate([a(L0_rec_tables), a(L0_rec_lin_sparse_w)[:, :, None]], axis=2).reshape(M * V, ROW),
        "dense_t": np.ascontiguousarray(a(r_dense).T),
        "w1a": tiles(conv1[:, first, second].T),
        "w1b": tiles(conv1[:, second, first].T),
        "w1_fix": tiles(fix),
        "w2": np.ascontiguousarray(conv2.transpose(3, 1, 2, 0).reshape(P, T2, HALF)),
        "mlp1": a(L0_rec_W1), "mlp2": a(L0_rec_W2), "mlp3": a(L0_rec_W3),
        "small": small,
        "sel1": np.ascontiguousarray(sel1.reshape(XR, UT, UK)),
        "sel2": np.ascontiguousarray(sel2.reshape(XR, T2, P)),
        "ident": np.eye(P, dtype=f32),
        "ident_bf": np.eye(P, dtype=f32).astype(bf),
    }
    nc = bacc.Bacc("TRN2", target_bir_lowering=False, num_devices=1)
    args = {k: nc.dram_tensor(f"in_{k}", v.shape, mybir.dt.from_np(v.dtype), kind="ExternalInput").ap()
            for k, v in arrays.items()}
    out = nc.dram_tensor("out_row", (B,), F32, kind="ExternalOutput").ap()
    build(nc, out=out, **args)
    r = run_bass_kernel_spmd(nc, [{f"in_{k}": v for k, v in arrays.items()}], core_ids=[0])
    return r.results[0]["out_row"]
```

```python
from contextlib import ExitStack

import concourse.bass as bass
from concourse import mybir

F32 = mybir.dt.float32
F32R = mybir.dt.float32r
BF16 = mybir.dt.bfloat16
I32 = mybir.dt.int32
U32 = mybir.dt.uint32
ALU = mybir.AluOpType
ACT = mybir.ActivationFunctionType
AX = mybir.AxisListType

P = 128
B, M, V, E, ND = 512, 26, 1250, 32, 13
BT = B // P
ROW = E + 1
HALF = 64
CH = 512
NPAIR = B * E // (2 * CH)
GP = NPAIR // BT
DP = E // GP
NPR = M * (M + 1) // 2
UT = 3
UK = NPR // UT
T2 = M * HALF // P
XR = 3 * M
D1, D2, D3 = 1024, 512, 256
K1 = 7
K1_LAST = M * E + ND - (K1 - 1) * P
EMB_LAST = M * E - (K1 - 1) * P
K2, K3 = D1 // P, D2 // P
WP = 1024
SUMS_B, SUMS_A = (0, 1, 2), (6, 7, 8)
TURN_AT = 3
LOW_B, LOW_A = (3, 4, 5), (9, 10, 11)
L1_B, L1_A = (4, 5, 6), (10, 11, 12)
ADD2_AT, ADD1_AT = 7, 12
SPLIT_AT = (6, 8, 10, 12)
C_B1, C_B2, C_B3, C_DEEP, C_CB1, C_CB2, C_CIN1, C_CIN2, C_AUX, C_END = 0, 8, 12, 14, 16, 17, 18, 19, 20, 21



def build(nc, idx, idx_base, table, dense_t, w1a, w1b, w1_fix, w2, mlp1, mlp2, mlp3, small, sel1, sel2,
          ident, ident_bf, out):
    with ExitStack() as ctx:
        def sb(name, shape, dt=F32):
            return ctx.enter_context(nc.sbuf_tensor(name, shape, dt))

        def ps(name, shape, dt=F32):
            return ctx.enter_context(nc.psum_tensor(name, shape, dt))

        def sem(name):
            return ctx.enter_context(nc.semaphore(name))

        small_sb = sb("small_sb", [P, C_END])
        sel1_sb = sb("sel1_sb", [XR, UT, UK], BF16)
        sel2_sb = sb("sel2_sb", [XR, T2, P], BF16)
        ident_sb = sb("ident_sb", [P, P])
        identb_sb = sb("identb_sb", [P, P], BF16)
        w1_hi = sb("w1_hi", [UK, UT, P], F32R)
        w1_lo = sb("w1_lo", [UK, UT, P], F32R)
        w2_sb = sb("w2_sb", [P, T2, HALF])
        m1_hi = sb("m1_hi", [P, K1, D1], F32R)
        m1_lo = sb("m1_lo", [P, K1, D1], F32R)
        m2_hi = sb("m2_hi", [P, K2, D2], F32R)
        m2_lo = sb("m2_lo", [P, K2, D2], F32R)
        m3_hi = sb("m3_hi", [P, K3, D3], F32R)
        m3_lo = sb("m3_lo", [P, K3, D3], F32R)
        rows = sb("rows", [P, BT, M], U32)
        emb = sb("emb", [P, BT, M, ROW])
        res1 = [sb(f"res1_{k}", [P, CH]) for k in range(2)]
        res2 = [sb(f"res2_{k}", [P, CH]) for k in range(2)]
        with ExitStack() as sums_of_d:
            acc1 = sums_of_d.enter_context(nc.sbuf_tensor("acc1", [P, BT, CH], F32))
            acc2 = sums_of_d.enter_context(nc.sbuf_tensor("acc2", [P, BT + 1, CH], F32))
        h1_lo = sb("h1_lo", [P, 2 * BT + 1, CH], F32R)[:, 0:K2, :]
        aux = sb("aux", [P, B])
        lin = sb("lin", [P, BT])
        with ExitStack() as early:
            idx_sb = early.enter_context(nc.sbuf_tensor("idx_sb", [P, BT, M], I32))
            base_sb = early.enter_context(nc.sbuf_tensor("base_sb", [P, BT, M], I32))
            wrap = early.enter_context(nc.sbuf_tensor("wrap", [P, BT, M], F32))
            inside = early.enter_context(nc.sbuf_tensor("inside", [P, BT, M], F32))
            clamped = early.enter_context(nc.sbuf_tensor("clamped", [P, BT, M], F32))
            w1a_sb = early.enter_context(nc.sbuf_tensor("w1a_sb", [UK, UT, P], F32))
            w1b_sb = early.enter_context(nc.sbuf_tensor("w1b_sb", [UK, UT, P], F32))
            fix_sb = early.enter_context(nc.sbuf_tensor("fix_sb", [UK, UT, M], F32))
        prod = [sb(f"prod{k}", [P, 2, CH]) for k in range(2)]
        with ExitStack() as cin:
            rest = cin.enter_context(nc.sbuf_tensor("rest", [P, M, E], F32))
            parts = cin.enter_context(nc.sbuf_tensor("parts", [P, E, 3, M], BF16))
            sq = cin.enter_context(nc.sbuf_tensor("sq", [UK, UT, CH], F32))
            sq_hi = cin.enter_context(nc.sbuf_tensor("sq_hi", [UK, UT, CH], F32R))
            sq_lo = cin.enter_context(nc.sbuf_tensor("sq_lo", [UK, UT, CH], F32R))
            x = [cin.enter_context(nc.sbuf_tensor(f"x{k}", [XR, 2 * CH], BF16)) for k in range(4)]
            xk = [cin.enter_context(nc.sbuf_tensor(f"xk{k}", [P, 2, CH], F32)) for k in range(2)]
            wpiece = [cin.enter_context(nc.sbuf_tensor(f"wpiece{k}", [P, WP], F32)) for k in range(2)]
        xt_hi = sb("xt_hi", [P, K1, B], F32R)
        xt_lo = sb("xt_lo", [P, K1, B], F32R)
        h1_hi = sb("h1_hi", [P, K2, B], F32R)
        packed = [w[:, 0:B].rearrange("p (t n) -> p t n", t=BT) for w in wpiece]
        h2_hi, h2_lo = xt_hi, xt_lo
        hf = [prod[0][:, k, :] for k in range(2)]
        h3 = prod[1]
        fold1 = res1[0][:, :].rearrange("p (t b) -> p t b", t=BT)
        fold2 = res1[1][:, :].rearrange("p (t b) -> p t b", t=BT)
        row_sb = res2[0][0:1, :]

        spread = [ps(f"spread{k}", [P, 2, CH]) for k in range(2)]
        l2out = [ps(f"l2out{k}", [P, CH]) for k in range(2)]
        l1out = ps("l1out", [P, CH])
        stage = ps("stage", [P, CH])
        stage_bf = stage[:, :].bitcast(BF16)
        row_ps = l2out[0]

        idx_in, base_in, small_in = sem("idx_in"), sem("base_in"), sem("small_in")
        w1_in, w2_in, sel_in, ident_in, dense_in = (sem("w1_in"), sem("w2_in"), sem("sel_in"),
                                                    sem("ident_in"), sem("dense_in"))
        piece_in = [sem("piece_in0"), sem("piece_in1")]
        piece_hi, piece_lo = sem("piece_hi"), sem("piece_lo")
        idx_step = sem("idx_step")
        emb_in = sem("emb_in")
        zeroed = sem("zeroed")
        w1_step = sem("w1_step")
        fix_done = sem("fix_done")
        split_step = sem("split_step")
        turned = sem("turned")
        x_ready = sem("x_ready")
        sums_done = sem("sums_done")
        hi_done = sem("hi_done")
        lo_done = sem("lo_done")
        l1_done = sem("l1_done")
        l1_read = sem("l1_read")
        xk_ready = sem("xk_ready")
        spread_done = sem("spread_done")
        prod_done = sem("prod_done")
        main_done = sem("main_done")
        res2_ready = sem("res2_ready")
        add1_done, add2_done = sem("add1_done"), sem("add2_done")
        pack_done = sem("pack_done")
        xt_done, xt_hi_done, xt_lo_done = sem("xt_done"), sem("xt_hi_done"), sem("xt_lo_done")
        dense_split = sem("dense_split")
        mlp_done = sem("mlp_done")
        tanh_done, h_hi_done, h_lo_done = sem("tanh_done"), sem("h_hi_done"), sem("h_lo_done")
        fold_step = sem("fold_step")
        row_done, row_read, out_done = sem("row_done"), sem("row_read"), sem("out_done")

        NTILE = NPAIR * T2
        PIECES = K1 + K2 // 2 + 1
        ROWS_IN = 16 * M
        MLP_BANKS = [l1out, stage]
        MT = [D1 // P, D2 // P, D3 // P]
        HT = sum(MT)

        def slot(g, t):
            return g * T2 + t

        block = ctx.enter_context(nc.Block())

        @block.sync
        def _(sp):
            sp.dma_start(idx_sb[:, :, :], idx.rearrange("(t p) m -> p t m", p=P)).then_inc(idx_in, 16)
            sp.dma_start(base_sb[:, :, :], idx_base).then_inc(base_in, 16)
            sp.dma_start(w1a_sb[:, :, :], w1a).then_inc(w1_in, 16)
            sp.dma_start(w1b_sb[:, :, :], w1b).then_inc(w1_in, 16)
            sp.dma_start(fix_sb[:, :, :], w1_fix).then_inc(w1_in, 16)
            sp.dma_start(identb_sb[:, :], ident_bf).then_inc(ident_in, 16)
            sp.dma_start(ident_sb[:, :], ident).then_inc(ident_in, 16)
            sp.dma_start(sel1_sb[:, :, :], sel1).then_inc(sel_in, 16)
            sp.dma_start(sel2_sb[:, :, :], sel2).then_inc(sel_in, 16)
            sp.dma_start(small_sb[:, :], small).then_inc(small_in, 16)
            sp.dma_start(w2_sb[:, :, :], w2).then_inc(w2_in, 16)
            sp.wait_ge(zeroed, 1)
            sp.dma_start(aux[EMB_LAST:EMB_LAST + ND, :], dense_t).then_inc(dense_in, 16)
            for k in range(PIECES):
                if k >= 2:
                    sp.wait_ge(piece_lo, k - 1)
                if k < K1:
                    n = P if k < K1 - 1 else K1_LAST
                    dst, src = wpiece[k % 2][0:n, :], mlp1[k * P:k * P + n, :]
                elif k < PIECES - 1:
                    j = 2 * (k - K1)
                    dst = wpiece[k % 2][:, :].rearrange("p (k n) -> p k n", k=2)
                    src = mlp2[j * P:(j + 2) * P, :].rearrange("(k p) n -> p k n", p=P)
                else:
                    dst = wpiece[k % 2][:, :].rearrange("p (k n) -> p k n", k=K3)
                    src = mlp3.rearrange("(k p) n -> p k n", p=P)
                sp.dma_start(dst, src).then_inc(piece_in[k % 2], 16)
            sp.wait_ge(row_read, 1)
            sp.dma_start(out.rearrange("(a b) -> a b", a=1), row_sb).then_inc(out_done, 16)
            sp.wait_ge(out_done, 16)

        @block.gpsimd
        def _(pool):
            pool.wait_ge(idx_step, 5)
            for b in range(BT):
                for m in range(M):
                    pool.indirect_dma_start(
                        out=emb[:, b, m, :], out_offset=None, in_=table,
                        in_offset=bass.IndirectOffsetOnAxis(ap=rows[:, b, m:m + 1], axis=0),
                    ).then_inc(emb_in, 16)
                pool.wait_ge(emb_in, ROWS_IN * (b + 1))
            for k in range(PIECES):
                n = K1_LAST if k == K1 - 1 else P
                if k < K1:
                    hi, lo = m1_hi[0:n, k, :], m1_lo[0:n, k, :]
                elif k < PIECES - 1:
                    j = 2 * (k - K1)
                    hi = m2_hi[:, j:j + 2, :].rearrange("p k n -> p (k n)")
                    lo = m2_lo[:, j:j + 2, :].rearrange("p k n -> p (k n)")
                else:
                    hi = m3_hi[:, :, :].rearrange("p k n -> p (k n)")
                    lo = m3_lo[:, :, :].rearrange("p k n -> p (k n)")
                pool.wait_ge(piece_in[k % 2], 16 * (k // 2 + 1))
                nc.gpsimd.tensor_copy(hi, wpiece[k % 2][0:n, :]).then_inc(piece_hi, 1)
                pool.wait_ge(piece_hi, k + 1)
                nc.gpsimd.tensor_tensor(lo, wpiece[k % 2][0:n, :], hi.bitcast(F32),
                                        ALU.subtract).then_inc(piece_lo, 1)

            pool.wait_ge(piece_lo, PIECES)
            for k in range(K1):
                n = (P if k < K1 - 1 else EMB_LAST) // E
                if k >= 2:
                    pool.wait_ge(xt_done, k - 1)
                nc.gpsimd.tensor_copy(packed[k % 2][:, :, 0:n * E].rearrange("p t (m d) -> p t m d", d=E),
                                      emb[:, :, 4 * k:4 * k + n, 0:E]).then_inc(pack_done, 1)

        @block.tensor
        def _(pe):
            def turn(g):
                for d in range(DP):
                    mm = nc.tensor.transpose(stage_bf[0:XR, d * P:(d + 1) * P],
                                             parts[:, g * DP + d, :, :].rearrange("p a m -> p (a m)"),
                                             identb_sb[:, :])
                mm.then_inc(turned, 1)

            def sums(u, xp, c):
                nc.tensor.matmul(stage[0:UK, :], sel1_sb[:, u, :], xp[:, c * CH:(c + 1) * CH],
                                 start=True, stop=True).then_inc(sums_done, 1)

            def layer1(chunk, u):
                pe.wait_ge(lo_done, UT * chunk + u + 1)
                if u == 0 and not (isinstance(chunk, int) and chunk == 0):
                    pe.wait_ge(l1_read, chunk)
                for k, (w, s) in enumerate(((w1_hi, sq_hi), (w1_lo, sq_hi), (w1_hi, sq_lo))):
                    mm = nc.tensor.matmul(l1out[:, :], w[:, u, :], s[:, u, :],
                                          start=(u == 0 and k == 0), stop=(u == UT - 1 and k == 2))
                mm.then_inc(l1_done, 1)

            def spread_tile(t, k, xp):
                for c in range(2):
                    mm = nc.tensor.matmul(spread[k % 2][:, c, :], sel2_sb[:, t, :],
                                          xp[:, c * CH:(c + 1) * CH], start=True, stop=True)
                mm.then_inc(spread_done, 1)

            def main(t, k, lo):
                for c in range(2):
                    mm = nc.tensor.matmul(lo[c * HALF:(c + 1) * HALF, :], w2_sb[:, t, :],
                                          prod[k % 2][:, c, :], start=(t == 0), stop=(t == T2 - 1))
                mm.then_inc(main_done, 1)

            def turn_embeddings(k):
                if k:
                    pe.wait_ge(xt_lo_done, k)
                pe.wait_ge(pack_done, k + 1)
                n = P if k < K1 - 1 else EMB_LAST
                for b in range(BT):
                    mm = nc.tensor.transpose(stage[0:n, b * P:(b + 1) * P],
                                             packed[k % 2][:, b, 0:n], ident_sb[:, :])
                mm.then_inc(xt_done, 1)

            def pairs(b, last):
                for g in range(GP):
                    i = b * GP + g
                    end = last and g == GP - 1
                    nxt, after = x[(g + 1) % 4], x[(g + 2) % 4]
                    two_on = not (last and g >= 2)
                    for t in range(T2):
                        k = slot(g, t)
                        pe.wait_ge(prod_done, i * T2 + t + 1)
                        main(t, k, l2out[g % 2])
                        if t + 2 < T2:
                            spread_tile(t + 2, k + 2, x[g])
                        elif not end:
                            spread_tile(t + 2 - T2, k + 2, nxt)
                        if end:
                            if t % 2 == 0:
                                if t == 0:
                                    pe.wait_ge(hi_done, UT * 2 * NPAIR)
                                turn_embeddings(t // 2)
                            continue
                        if t in L1_B:
                            layer1(2 * i + 3, L1_B.index(t))
                        if t in L1_A and two_on:
                            layer1(2 * i + 4, L1_A.index(t))
                        if t in SUMS_B:
                            u = SUMS_B.index(t)
                            pe.wait_ge(hi_done, UT * (2 * i + 3) + u)
                            sums(u, nxt, 1)
                        if t == TURN_AT and two_on:
                            pe.wait_ge(split_step, 4 * (b + (1 if g < 2 else 2)))
                            pe.wait_ge(hi_done, UT * (2 * i + 4))
                            turn((g + 2) % 4)
                        if t in SUMS_A and two_on:
                            u = SUMS_A.index(t)
                            if u == 0:
                                pe.wait_ge(x_ready, i + 3)
                            else:
                                pe.wait_ge(hi_done, UT * (2 * i + 4) + u)
                            sums(u, after, 0)

            pe.wait_ge(w1_in, 48)
            pe.wait_ge(w1_step, 2)
            for u in range(UT):
                mm = nc.tensor.matmul(l1out[0:M, 0:P], fix_sb[:, u, :], w1a_sb[:, u, :],
                                      start=(u == 0), stop=(u == UT - 1))
            mm.then_inc(fix_done, 1)
            pe.wait_ge(ident_in, 32)
            pe.wait_ge(split_step, 4)
            turn(0)
            pe.wait_ge(x_ready, 1)
            turn(1)
            pe.wait_ge(sel_in, 32)
            pe.wait_ge(x_ready, 2)
            for chunk in range(3):
                for u in range(UT):
                    if chunk + u:
                        pe.wait_ge(hi_done, UT * chunk + u)
                    sums(u, x[chunk // 2], chunk % 2)
                if chunk == 0:
                    pe.wait_ge(w1_step, 5)
                for u in range(UT):
                    layer1(chunk, u)
            pe.wait_ge(w2_in, 16)
            spread_tile(0, 0, x[0])
            spread_tile(1, 1, x[0])

            with pe.Fori(0, BT - 1) as b:
                pairs(b, False)
            pairs(BT - 1, True)

            pe.wait_ge(piece_lo, PIECES)
            pe.wait_ge(dense_split, 2)
            pe.wait_ge(xt_lo_done, K1)
            pe.wait_ge(l1_read, 2 * NPAIR)
            n = 0
            for layer, (hi, lo, kt, xh, xl) in enumerate((
                    (m1_hi, m1_lo, K1, xt_hi, xt_lo), (m2_hi, m2_lo, K2, h1_hi, h1_lo),
                    (m3_hi, m3_lo, K3, h2_hi, h2_lo))):
                before = sum(MT[:layer])
                for mt in range(MT[layer]):
                    if n >= 2:
                        pe.wait_ge(tanh_done, n - 1)
                    for k in range(kt):
                        if layer and mt == 0:
                            pe.wait_ge(h_lo_done, before - kt + k + 1)
                        r = K1_LAST if layer == 0 and k == K1 - 1 else P
                        for j, (w, h) in enumerate(((hi, xh), (lo, xh), (hi, xl))):
                            mm = nc.tensor.matmul(MLP_BANKS[n % 2][:, :], w[0:r, k, mt * P:(mt + 1) * P],
                                                  h[0:r, k, :], start=(k == 0 and j == 0),
                                                  stop=(k == kt - 1 and j == 2))
                    mm.then_inc(mlp_done, 1)
                    n += 1
                if layer == 0:
                    pe.wait_ge(fold_step, 6)
                    pe.wait_ge(small_in, 16)
                    pe.wait_ge(dense_in, 16)
                    pe.wait_ge(res2_ready, NPAIR + 1)
                    row = row_ps[0:1, :]
                    nc.tensor.matmul(row, small_sb[:, C_AUX:C_AUX + 1], aux[:, :], start=True, stop=False)
                    for c, f in ((C_CIN1, fold1), (C_CIN2, fold2)):
                        nc.tensor.matmul(row, small_sb[:, c:c + 1], f[:, :, :].rearrange("p t b -> p (t b)"),
                                         start=False, stop=False)
                    for t in range(BT):
                        nc.tensor.matmul(row_ps[0:1, t * P:(t + 1) * P], lin[:, t:t + 1], ident_sb[:, :],
                                         start=False, stop=False, skip_group_check=True)
            for k in range(D3 // P):
                pe.wait_ge(tanh_done, HT - D3 // P + k + 1)
                mm = nc.tensor.matmul(row_ps[0:1, :], small_sb[:, C_DEEP + k:C_DEEP + k + 1], h3[:, k, :],
                                      start=False, stop=(k == D3 // P - 1))
            mm.then_inc(row_done, 1)

        @block.scalar
        def _(act):
            def copy_x(pair, k):
                act.wait_ge(turned, pair + 1)
                nc.scalar.activation(x[k][:, :], stage_bf[0:XR, :], ACT.Copy).then_inc(x_ready, 1)

            def squares(chunk, u):
                act.wait_ge(sums_done, chunk * UT + u + 1)
                if not (isinstance(chunk, int) and chunk == 0):
                    act.wait_ge(l1_done, (chunk - 1) * UT + u + 1)
                nc.scalar.activation(sq[:, u, :], stage[0:UK, :], ACT.Square)
                nc.scalar.activation(sq_hi[:, u, :], stage[0:UK, :], ACT.Square).then_inc(hi_done, 1)

            def sigmoid(chunk, c, k, q):
                if q == 0:
                    act.wait_ge(l1_done, UT * (chunk + 1))
                if q < 2:
                    nc.scalar.activation(xk[k][q * HALF:(q + 1) * HALF, c, :], l1out[0:HALF, :], ACT.Sigmoid,
                                         bias=small_sb[0:HALF, C_CB1:C_CB1 + 1]).then_inc(xk_ready, 1)
                else:
                    nc.scalar.activation(res1[k][c * HALF:(c + 1) * HALF, :], l1out[HALF:P, :], ACT.Sigmoid,
                                         bias=small_sb[HALF:P, C_CB1:C_CB1 + 1]).then_inc(l1_read, 1)

            def pairs(b, last):
                for g in range(GP):
                    i = b * GP + g
                    end = last and g == GP - 1
                    if not end:
                        for u in range(UT):
                            squares(2 * i + 3, u)
                            if u == 0:
                                act.wait_ge(prod_done, i * T2 + 1)
                            sigmoid(2 * i + 2, 0, (g + 1) % 2, u)
                        two_on = not (last and g >= 2)
                        if two_on:
                            copy_x(i + 2, (g + 2) % 4)
                        for u in range(UT):
                            if two_on:
                                squares(2 * i + 4, u)
                            sigmoid(2 * i + 3, 1, (g + 1) % 2, u)
                    else:
                        act.wait_ge(dense_in, 16)
                        nc.scalar.activation(xt_hi[EMB_LAST:EMB_LAST + ND, K1 - 1, :],
                                             aux[EMB_LAST:EMB_LAST + ND, :], ACT.Copy).then_inc(dense_split, 1)
                        for k in range(K1):
                            n = P if k < K1 - 1 else EMB_LAST
                            act.wait_ge(xt_done, k + 1)
                            nc.scalar.activation(xt_hi[0:n, k, :], stage[0:n, :], ACT.Copy)\
                              .then_inc(xt_hi_done, 1)
                    act.wait_ge(main_done, (i + 1) * T2)
                    nc.scalar.activation(res2[g % 2][:, :], l2out[g % 2][:, :], ACT.Sigmoid,
                                         bias=small_sb[:, C_CB2:C_CB2 + 1]).then_inc(res2_ready, 1)

            for k in range(2):
                copy_x(k, k)
            act.wait_ge(small_in, 16)
            for chunk in range(3):
                for u in range(UT):
                    squares(chunk, u)
                if chunk < 2:
                    for q in range(3):
                        sigmoid(chunk, chunk, 0, q)

            with act.Fori(0, BT - 1) as b:
                pairs(b, False)
            pairs(BT - 1, True)

            n = 0
            for layer, bias in enumerate((C_B1, C_B2, C_B3)):
                for mt in range(MT[layer]):
                    act.wait_ge(mlp_done, n + 1)
                    if layer < 2 and n >= 2:
                        act.wait_ge(h_lo_done, n - 1)
                    dst = hf[n % 2] if layer < 2 else h3[:, mt, :]
                    nc.scalar.activation(dst, MLP_BANKS[n % 2][:, :], ACT.Tanh,
                                         bias=small_sb[:, bias + mt:bias + mt + 1]).then_inc(tanh_done, 1)
                    n += 1

        @block.vector
        def _(dve):
            def split(b, step):
                e = emb[:, bass.ds(b, 1), :, 0:E].rearrange("p t m d -> p (t m) d") if not isinstance(b, int) \
                    else emb[:, b, :, 0:E]
                part = [parts[:, :, j, :].rearrange("p d m -> p m d") for j in range(3)]
                if step == 0:
                    ins = nc.vector.tensor_copy(part[0], e)
                elif step == 1:
                    ins = nc.vector.tensor_tensor(rest[:, :, :], e, part[0], ALU.subtract)
                elif step == 2:
                    ins = nc.vector.tensor_copy(part[1], rest[:, :, :])
                else:
                    ins = nc.vector.tensor_tensor(part[2], rest[:, :, :], part[1], ALU.subtract)
                ins.then_inc(split_step, 1)

            def low(tile, u):
                dve.wait_ge(hi_done, tile + 1)
                nc.vector.tensor_tensor(sq_lo[:, u, :], sq[:, u, :], sq_hi[:, u, :].bitcast(F32),
                                        ALU.subtract).then_inc(lo_done, 1)

            def block_of(a, b, off):
                if isinstance(b, int):
                    return a[:, b + off, :]
                return a[:, bass.ds(b + off, 1), :].rearrange("p t n -> p (t n)")

            def pairs(b, last):
                for g in range(GP):
                    i = b * GP + g
                    end = last and g == GP - 1
                    for t in range(T2):
                        k = slot(g, t)
                        dve.wait_ge(spread_done, i * T2 + t + 1)
                        if t == 0:
                            dve.wait_ge(xk_ready, 4 * (i + 1))
                        nc.vector.tensor_tensor(prod[k % 2][:, :, :].rearrange("p c n -> p (c n)"),
                                                spread[k % 2][:, :, :].rearrange("p c n -> p (c n)"),
                                                xk[g % 2][:, :, :].rearrange("p c n -> p (c n)"),
                                                ALU.mult).then_inc(prod_done, 1)
                        if t in LOW_B and not end:
                            u = LOW_B.index(t)
                            low(UT * (2 * i + 3) + u, u)
                        if t in LOW_A and not (last and g >= 2):
                            u = LOW_A.index(t)
                            low(UT * (2 * i + 4) + u, u)
                        if t == ADD1_AT:
                            dve.wait_ge(l1_read, 2 * (i + 1))
                            a = block_of(acc1, b, 0)
                            nc.vector.tensor_tensor(a, a, res1[g % 2][:, :], ALU.add).then_inc(add1_done, 1)
                        if t == ADD2_AT:
                            dve.wait_ge(res2_ready, i + 1)
                            a = block_of(acc2, b, 0 if g == 0 else 1)
                            nc.vector.tensor_tensor(a, a, res2[(g + 1) % 2][:, :], ALU.add)\
                              .then_inc(add2_done, 1)
                        if g == 1 and not last and t in SPLIT_AT:
                            step = SPLIT_AT.index(t)
                            if step == 0:
                                dve.wait_ge(emb_in, ROWS_IN * (b + 2))
                                dve.wait_ge(turned, 4 * (b + 1))
                            else:
                                dve.wait_ge(split_step, 4 * (b + 1) + step)
                            split(b + 1, step)
                        if end and t % 2 == 0:
                            tile = t // 2
                            n = P if tile < K1 - 1 else EMB_LAST
                            dve.wait_ge(xt_hi_done, tile + 1)
                            nc.vector.tensor_tensor(xt_lo[0:n, tile, :], stage[0:n, :],
                                                    xt_hi[0:n, tile, :].bitcast(F32), ALU.subtract)\
                              .then_inc(xt_lo_done, 1)

            dve.wait_ge(idx_in, 16)
            nc.vector.tensor_scalar(wrap[:, :, :], idx_sb[:, :, :], 0.0, float(V), ALU.is_lt, ALU.mult)\
              .then_inc(idx_step, 1)
            dve.wait_ge(idx_step, 1)
            nc.vector.tensor_tensor(inside[:, :, :], idx_sb[:, :, :], wrap[:, :, :], ALU.add).then_inc(idx_step, 1)
            dve.wait_ge(idx_step, 2)
            nc.vector.tensor_scalar(clamped[:, :, :], inside[:, :, :], 0.0, float(V - 1), ALU.max, ALU.min)\
              .then_inc(idx_step, 1)
            dve.wait_ge(base_in, 16)
            dve.wait_ge(idx_step, 3)
            nc.vector.tensor_tensor(rows[:, :, :], clamped[:, :, :], base_sb[:, :, :], ALU.add).then_inc(idx_step, 2)
            nc.vector.memset(aux[:, :], 1.0).then_inc(zeroed, 1)
            nc.vector.memset(acc1[:, :, :], 0.0).then_inc(zeroed, 1)
            nc.vector.memset(acc2[:, :, :], 0.0).then_inc(zeroed, 1)
            nc.vector.memset(res2[1][:, :], 0.0).then_inc(res2_ready, 1)
            dve.wait_ge(w1_in, 48)
            nc.vector.tensor_tensor(w1b_sb[:, :, :], w1a_sb[:, :, :], w1b_sb[:, :, :], ALU.add).then_inc(w1_step, 1)
            dve.wait_ge(w1_step, 1)
            nc.vector.tensor_scalar(w1a_sb[:, :, :], w1b_sb[:, :, :], 0.5, None, ALU.mult).then_inc(w1_step, 1)
            dve.wait_ge(fix_done, 1)
            nc.vector.tensor_copy(w1a_sb[0:M, 0, :], l1out[0:M, 0:P]).then_inc(w1_step, 1)
            dve.wait_ge(w1_step, 3)
            nc.vector.tensor_copy(w1_hi[:, :, :], w1a_sb[:, :, :]).then_inc(w1_step, 1)
            dve.wait_ge(w1_step, 4)
            nc.vector.tensor_tensor(w1_lo[:, :, :], w1a_sb[:, :, :], w1_hi[:, :, :].bitcast(F32),
                                    ALU.subtract).then_inc(w1_step, 1)
            dve.wait_ge(zeroed, 3)
            dve.wait_ge(emb_in, ROWS_IN)
            for step in range(4):
                if step:
                    dve.wait_ge(split_step, step)
                split(0, step)
            for tile in range(3 * UT):
                low(tile, tile % UT)

            with dve.Fori(0, BT - 1) as b:
                pairs(b, False)
            pairs(BT - 1, True)

            dve.wait_ge(dense_split, 1)
            nc.vector.tensor_tensor(xt_lo[EMB_LAST:EMB_LAST + ND, K1 - 1, :], aux[EMB_LAST:EMB_LAST + ND, :],
                                    xt_hi[EMB_LAST:EMB_LAST + ND, K1 - 1, :].bitcast(F32), ALU.subtract)\
              .then_inc(dense_split, 1)
            nc.vector.tensor_reduce(lin[:, :], emb[:, :, :, E], AX.X, ALU.add).then_inc(fold_step, 1)
            dve.wait_ge(res2_ready, NPAIR + 1)
            nc.vector.tensor_tensor(acc2[:, BT, :], acc2[:, BT, :], res2[1][:, :], ALU.add).then_inc(fold_step, 1)
            dve.wait_ge(add1_done, NPAIR)
            dve.wait_ge(fold_step, 2)
            for a, f, n in ((acc1[:, :, :], fold1, 3), (acc2[:, 1:BT + 1, :], fold2, 5)):
                half = a[:, :, 0:2 * P]
                nc.vector.tensor_tensor(half, half, a[:, :, 2 * P:4 * P], ALU.add).then_inc(fold_step, 1)
                dve.wait_ge(fold_step, n)
                nc.vector.tensor_tensor(f[:, :, :], a[:, :, 0:P], a[:, :, P:2 * P], ALU.add)\
                  .then_inc(fold_step, 1)

            n = 0
            for layer, (hi, lo) in enumerate(((h1_hi, h1_lo), (h2_hi, h2_lo))):
                for mt in range(MT[layer]):
                    dve.wait_ge(tanh_done, n + 1)
                    if layer and mt == 0:
                        dve.wait_ge(mlp_done, MT[0])
                    nc.vector.tensor_copy(hi[:, mt, :], hf[n % 2]).then_inc(h_hi_done, 1)
                    dve.wait_ge(h_hi_done, n + 1)
                    nc.vector.tensor_tensor(lo[:, mt, :], hf[n % 2], hi[:, mt, :].bitcast(F32),
                                            ALU.subtract).then_inc(h_lo_done, 1)
                    n += 1
            dve.wait_ge(row_done, 1)
            nc.vector.tensor_copy(row_sb, row_ps[0:1, :]).then_inc(row_read, 1)


def kernel(r_dense, r_sparse, L0_rec_tables, L0_rec_lin_sparse_w, L0_rec_lin_dense_w, L0_rec_conv1_w,
           L0_rec_conv1_b, L0_rec_conv2_w, L0_rec_conv2_b, L0_rec_cin_w, L0_rec_cin_b, L0_rec_W1, L0_rec_b1,
           L0_rec_W2, L0_rec_b2, L0_rec_W3, L0_rec_b3, L0_rec_deep_w, L0_rec_deep_b, L0_rec_bias):
    import ml_dtypes
    import numpy as np
    import concourse.bacc as bacc
    from concourse.bass_utils import run_bass_kernel_spmd

    a = np.asarray
    f32, bf = np.float32, ml_dtypes.bfloat16
    first = np.array([m for m in range(M)] + [m for m in range(M) for n in range(m + 1, M)])
    second = np.array([m for m in range(M)] + [n for m in range(M) for n in range(m + 1, M)])
    tiles = lambda w: np.ascontiguousarray(w.reshape(UT, UK, -1).transpose(1, 0, 2))
    conv1 = a(L0_rec_conv1_w).reshape(P, M, M)
    conv2 = a(L0_rec_conv2_w)[HALF:].reshape(HALF, HALF, T2, 2)
    pair_of = np.arange(NPR)
    sel1 = np.zeros((3, M, NPR), bf)
    sel1[:, first, pair_of] = 1
    sel1[:, second, pair_of] = 1
    sel2 = np.zeros((3, M, T2, 2, HALF), bf)
    fix = np.zeros((NPR, M), f32)
    fix[pair_of, first] = -1
    fix[pair_of, second] = -1
    fix[np.arange(M), np.arange(M)] = 1
    for t in range(T2):
        for j in range(2):
            sel2[:, 2 * t + j, t, j, :] = 1
    small = np.zeros((P, C_END), f32)
    small[:, C_B1:C_B2] = a(L0_rec_b1).reshape(-1, P).T
    small[:, C_B2:C_B3] = a(L0_rec_b2).reshape(-1, P).T
    small[:, C_B3:C_DEEP] = a(L0_rec_b3).reshape(-1, P).T
    small[:, C_DEEP:C_CB1] = a(L0_rec_deep_w).reshape(-1, P).T
    small[:, C_CB1] = a(L0_rec_conv1_b)
    for j in range(2):
        small[j * HALF:(j + 1) * HALF, C_CB2] = a(L0_rec_conv2_b)[HALF:]
        small[j * HALF:(j + 1) * HALF, C_CIN1] = a(L0_rec_cin_w)[:HALF, 0]
        small[j * HALF:(j + 1) * HALF, C_CIN2] = a(L0_rec_cin_w)[HALF:, 0]
    small[0, C_AUX], small[1, C_AUX], small[2, C_AUX] = a(L0_rec_cin_b)[0], a(L0_rec_deep_b)[0], a(L0_rec_bias)[0]
    small[EMB_LAST:EMB_LAST + ND, C_AUX] = a(L0_rec_lin_dense_w)

    arrays = {
        "idx": a(r_sparse),
        "idx_base": np.ascontiguousarray(np.broadcast_to(np.arange(M, dtype=np.int32) * V, (P, BT, M))),
        "table": np.concatenate([a(L0_rec_tables), a(L0_rec_lin_sparse_w)[:, :, None]], axis=2).reshape(M * V, ROW),
        "dense_t": np.ascontiguousarray(a(r_dense).T),
        "w1a": tiles(conv1[:, first, second].T),
        "w1b": tiles(conv1[:, second, first].T),
        "w1_fix": tiles(fix),
        "w2": np.ascontiguousarray(conv2.transpose(3, 1, 2, 0).reshape(P, T2, HALF)),
        "mlp1": a(L0_rec_W1), "mlp2": a(L0_rec_W2), "mlp3": a(L0_rec_W3),
        "small": small,
        "sel1": np.ascontiguousarray(sel1.reshape(XR, UT, UK)),
        "sel2": np.ascontiguousarray(sel2.reshape(XR, T2, P)),
        "ident": np.eye(P, dtype=f32),
        "ident_bf": np.eye(P, dtype=f32).astype(bf),
    }
    nc = bacc.Bacc("TRN2", target_bir_lowering=False, num_devices=1)
    args = {k: nc.dram_tensor(f"in_{k}", v.shape, mybir.dt.from_np(v.dtype), kind="ExternalInput").ap()
            for k, v in arrays.items()}
    out = nc.dram_tensor("out_row", (B,), F32, kind="ExternalOutput").ap()
    build(nc, out=out, **args)
    r = run_bass_kernel_spmd(nc, [{f"in_{k}": v for k, v in arrays.items()}], core_ids=[0])
    return r.results[0]["out_row"]
```

```python
from contextlib import ExitStack

import concourse.bass as bass
from concourse import mybir

F32 = mybir.dt.float32
F32R = mybir.dt.float32r
BF16 = mybir.dt.bfloat16
I32 = mybir.dt.int32
U32 = mybir.dt.uint32
ALU = mybir.AluOpType
ACT = mybir.ActivationFunctionType
AX = mybir.AxisListType

P = 128
B, M, V, E, ND = 512, 26, 1250, 32, 13
BT = B // P
ROW = E + 1
HALF = 64
CH = 512
NPAIR = B * E // (2 * CH)
GP = NPAIR // BT
DP = E // GP
NPR = M * (M + 1) // 2
UT = 3
UK = NPR // UT
T2 = M * HALF // P
XR = 3 * M
D1, D2, D3 = 1024, 512, 256
K1 = 7
EMB_LAST = M * ROW - (K1 - 1) * P
DENSE_AT = 96
K1_LAST = DENSE_AT + ND
K2, K3 = D1 // P, D2 // P
FIRST = 20
WP = 1024
SUMS_B, SUMS_A = (0, 1, 2), (6, 7, 8)
TURN_AT = 3
LOW_B, LOW_A = (3, 4, 5), (9, 10, 11)
L1_B, L1_A = (4, 5, 6), (10, 11, 12)
ADD2_AT, ADD1_AT = 7, 12
TURN_E = (0, 2, 3, 5, 7, 9, 10)
SPLIT_AT = (6, 8, 10, 12)
C_B1, C_B2, C_B3, C_DEEP, C_CB1, C_CB2, C_CIN1, C_CIN2, C_AUX, C_END = 0, 8, 12, 14, 16, 17, 18, 19, 20, 21



def build(nc, idx, idx_base, table, dense_t, w1a, w1b, w1_fix, w2, mlp1, mlp2, mlp3, small, sel1, sel2,
          ident, ident_bf, out):
    with ExitStack() as ctx:
        def sb(name, shape, dt=F32):
            return ctx.enter_context(nc.sbuf_tensor(name, shape, dt))

        def ps(name, shape, dt=F32):
            return ctx.enter_context(nc.psum_tensor(name, shape, dt))

        def sem(name):
            return ctx.enter_context(nc.semaphore(name))

        small_sb = sb("small_sb", [P, C_END])
        sel1_sb = sb("sel1_sb", [XR, UT, UK], BF16)
        sel2_sb = sb("sel2_sb", [XR, T2, P], BF16)
        ident_sb = sb("ident_sb", [P, P])
        identb_sb = sb("identb_sb", [P, P], BF16)
        w1_hi = sb("w1_hi", [UK, UT, P], F32R)
        w1_lo = sb("w1_lo", [UK, UT, P], F32R)
        w2_sb = sb("w2_sb", [P, T2, HALF])
        m1_hi = sb("m1_hi", [P, K1, D1], F32R)
        m1_lo = sb("m1_lo", [P, K1, D1], F32R)
        m2_hi = sb("m2_hi", [P, K2, D2], F32R)
        m2_lo = sb("m2_lo", [P, K2, D2], F32R)
        m3_hi = sb("m3_hi", [P, K3, D3], F32R)
        m3_lo = sb("m3_lo", [P, K3, D3], F32R)
        rows = sb("rows", [P, BT, M], U32)
        emb = sb("emb", [P, BT, M, ROW])
        res1 = [sb(f"res1_{k}", [P, CH]) for k in range(2)]
        res2 = [sb(f"res2_{k}", [P, CH]) for k in range(2)]
        with ExitStack() as sums_of_d:
            acc1 = sums_of_d.enter_context(nc.sbuf_tensor("acc1", [P, BT, CH], F32))
            acc2 = sums_of_d.enter_context(nc.sbuf_tensor("acc2", [P, BT + 1, CH], F32))
        h1_lo = sb("h1_lo", [P, 2 * BT + 1, CH], F32R)[:, 0:K2, :]
        aux = sb("aux", [P, B])
        lin = sb("lin", [P, BT])
        with ExitStack() as early:
            idx_sb = early.enter_context(nc.sbuf_tensor("idx_sb", [P, BT, M], I32))
            base_sb = early.enter_context(nc.sbuf_tensor("base_sb", [P, BT, M], I32))
            wrap = early.enter_context(nc.sbuf_tensor("wrap", [P, BT, M], F32))
            inside = early.enter_context(nc.sbuf_tensor("inside", [P, BT, M], F32))
            clamped = early.enter_context(nc.sbuf_tensor("clamped", [P, BT, M], F32))
            w1a_sb = early.enter_context(nc.sbuf_tensor("w1a_sb", [UK, UT, P], F32))
            w1b_sb = early.enter_context(nc.sbuf_tensor("w1b_sb", [UK, UT, P], F32))
            fix_sb = early.enter_context(nc.sbuf_tensor("fix_sb", [UK, UT, M], F32))
        prod = [sb(f"prod{k}", [P, 2, CH]) for k in range(2)]
        with ExitStack() as cin:
            rest = cin.enter_context(nc.sbuf_tensor("rest", [P, M, E], F32))
            parts = cin.enter_context(nc.sbuf_tensor("parts", [P, E, 3, M], BF16))
            sq = cin.enter_context(nc.sbuf_tensor("sq", [UK, UT, CH], F32))
            sq_hi = cin.enter_context(nc.sbuf_tensor("sq_hi", [UK, UT, CH], F32R))
            sq_lo = cin.enter_context(nc.sbuf_tensor("sq_lo", [UK, UT, CH], F32R))
            x = [cin.enter_context(nc.sbuf_tensor(f"x{k}", [XR, 2 * CH], BF16)) for k in range(4)]
            xk = [cin.enter_context(nc.sbuf_tensor(f"xk{k}", [P, 2, CH], F32)) for k in range(2)]
            wpiece = [cin.enter_context(nc.sbuf_tensor(f"wpiece{k}", [P, WP], F32)) for k in range(2)]
        xt_hi = sb("xt_hi", [P, K1, B], F32R)
        xt_lo = sb("xt_lo", [P, K1, B], F32R)
        h1_hi = sb("h1_hi", [P, K2, B], F32R)
        h2_hi, h2_lo = xt_hi, xt_lo
        hf = [prod[0][:, k, :] for k in range(2)]
        h3 = prod[1]
        fold1 = res1[0][:, :].rearrange("p (t b) -> p t b", t=BT)
        fold2 = res1[1][:, :].rearrange("p (t b) -> p t b", t=BT)
        row_sb = res2[0][0:1, :]

        spread = [ps(f"spread{k}", [P, 2, CH]) for k in range(2)]
        l2out = [ps(f"l2out{k}", [P, CH]) for k in range(2)]
        l1out = ps("l1out", [P, CH])
        stage = ps("stage", [P, CH])
        stage_bf = stage[:, :].bitcast(BF16)
        row_ps = l2out[0]
        early_sums = [spread[0][:, 0, :], spread[0][:, 1, :], spread[1][:, 0, :], spread[1][:, 1, :],
                      l2out[1][:, :], stage[:, :], l2out[0][:, :], l2out[1][:, :], stage[:, :]]
        early_turn = l2out[0][:, :].bitcast(BF16)
        turn_banks = [stage, l1out]

        idx_in, base_in, small_in = sem("idx_in"), sem("base_in"), sem("small_in")
        w1_in, w2_in, sel_in, ident_in, dense_in = (sem("w1_in"), sem("w2_in"), sem("sel_in"),
                                                    sem("ident_in"), sem("dense_in"))
        piece_in = [sem("piece_in0"), sem("piece_in1")]
        piece_hi, piece_lo = sem("piece_hi"), sem("piece_lo")
        idx_step = sem("idx_step")
        first_in = sem("first_in")
        emb_in = sem("emb_in")
        zeroed = sem("zeroed")
        w1_step = sem("w1_step")
        fix_done = sem("fix_done")
        first_split = sem("first_split")
        split_step = sem("split_step")
        turned = sem("turned")
        x_ready = sem("x_ready")
        sums_done = sem("sums_done")
        hi_done = sem("hi_done")
        lo_done = sem("lo_done")
        l1_done = sem("l1_done")
        l1_read = sem("l1_read")
        xk_ready = sem("xk_ready")
        spread_done = sem("spread_done")
        prod_done = sem("prod_done")
        main_done = sem("main_done")
        res2_ready = sem("res2_ready")
        add1_done, add2_done = sem("add1_done"), sem("add2_done")
        pad_done = sem("pad_done")
        xt_done, xt_hi_done, xt_lo_done = sem("xt_done"), sem("xt_hi_done"), sem("xt_lo_done")
        dense_split = sem("dense_split")
        mlp_done = sem("mlp_done")
        tanh_done, h_hi_done, h_lo_done = sem("tanh_done"), sem("h_hi_done"), sem("h_lo_done")
        fold_step = sem("fold_step")
        row_done, row_read, out_done = sem("row_done"), sem("row_read"), sem("out_done")

        NTILE = NPAIR * T2
        PIECES = K1 + K2 // 2 + 1
        ROWS_IN = 16 * M
        ROWS_FIRST = 16 * FIRST
        MLP_BANKS = [l1out, stage]
        MT = [D1 // P, D2 // P, D3 // P]
        HT = sum(MT)

        def slot(g, t):
            return g * T2 + t

        block = ctx.enter_context(nc.Block())

        @block.sync
        def _(sp):
            sp.dma_start(idx_sb[:, :, :], idx.rearrange("(t p) m -> p t m", p=P)).then_inc(idx_in, 16)
            sp.dma_start(base_sb[:, :, :], idx_base).then_inc(base_in, 16)
            sp.dma_start(w1a_sb[:, :, :], w1a).then_inc(w1_in, 16)
            sp.dma_start(w1b_sb[:, :, :], w1b).then_inc(w1_in, 16)
            sp.dma_start(fix_sb[:, :, :], w1_fix).then_inc(w1_in, 16)
            sp.dma_start(identb_sb[:, :], ident_bf).then_inc(ident_in, 16)
            sp.dma_start(ident_sb[:, :], ident).then_inc(ident_in, 16)
            sp.dma_start(sel1_sb[:, :, :], sel1).then_inc(sel_in, 16)
            sp.dma_start(sel2_sb[:, :, :], sel2).then_inc(sel_in, 16)
            sp.dma_start(small_sb[:, :], small).then_inc(small_in, 16)
            sp.dma_start(w2_sb[:, :, :], w2).then_inc(w2_in, 16)
            sp.wait_ge(zeroed, 1)
            sp.dma_start(aux[DENSE_AT:K1_LAST, :], dense_t).then_inc(dense_in, 16)
            for k in range(PIECES):
                if k >= 2:
                    sp.wait_ge(piece_lo, k - 1)
                if k < K1:
                    n = P if k < K1 - 1 else K1_LAST
                    dst, src = wpiece[k % 2][0:n, :], mlp1[k * P:k * P + n, :]
                elif k < PIECES - 1:
                    j = 2 * (k - K1)
                    dst = wpiece[k % 2][:, :].rearrange("p (k n) -> p k n", k=2)
                    src = mlp2[j * P:(j + 2) * P, :].rearrange("(k p) n -> p k n", p=P)
                else:
                    dst = wpiece[k % 2][:, :].rearrange("p (k n) -> p k n", k=K3)
                    src = mlp3.rearrange("(k p) n -> p k n", p=P)
                sp.dma_start(dst, src).then_inc(piece_in[k % 2], 16)
            sp.wait_ge(row_read, 1)
            sp.dma_start(out.rearrange("(a b) -> a b", a=1), row_sb).then_inc(out_done, 16)
            sp.wait_ge(out_done, 16)

        @block.gpsimd
        def _(pool):
            pool.wait_ge(idx_step, 5)
            for b in range(BT):
                for m in range(M):
                    pool.indirect_dma_start(
                        out=emb[:, b, m, :], out_offset=None, in_=table,
                        in_offset=bass.IndirectOffsetOnAxis(ap=rows[:, b, m:m + 1], axis=0),
                    ).then_inc(first_in if b == 0 and m < FIRST else emb_in, 16)
                pool.wait_ge(emb_in, ROWS_IN * (b + 1) - ROWS_FIRST)
            for k in range(PIECES):
                n = K1_LAST if k == K1 - 1 else P
                if k < K1:
                    hi, lo = m1_hi[0:n, k, :], m1_lo[0:n, k, :]
                elif k < PIECES - 1:
                    j = 2 * (k - K1)
                    hi = m2_hi[:, j:j + 2, :].rearrange("p k n -> p (k n)")
                    lo = m2_lo[:, j:j + 2, :].rearrange("p k n -> p (k n)")
                else:
                    hi = m3_hi[:, :, :].rearrange("p k n -> p (k n)")
                    lo = m3_lo[:, :, :].rearrange("p k n -> p (k n)")
                pool.wait_ge(piece_in[k % 2], 16 * (k // 2 + 1))
                nc.gpsimd.tensor_copy(hi, wpiece[k % 2][0:n, :]).then_inc(piece_hi, 1)
                pool.wait_ge(piece_hi, k + 1)
                nc.gpsimd.tensor_tensor(lo, wpiece[k % 2][0:n, :], hi.bitcast(F32),
                                        ALU.subtract).then_inc(piece_lo, 1)

            pool.wait_ge(l1_done, 2 * NPAIR * UT)
            pool.wait_ge(piece_lo, PIECES)
            nc.gpsimd.memset(xt_hi[HALF:DENSE_AT, K1 - 1, :].bitcast(F32), 0.0).then_inc(pad_done, 1)
            pool.wait_ge(pad_done, 1)
            nc.gpsimd.memset(xt_lo[HALF:DENSE_AT, K1 - 1, :].bitcast(F32), 0.0).then_inc(pad_done, 1)

        @block.tensor
        def _(pe):
            def turn(g, dst):
                for d in range(DP):
                    mm = nc.tensor.transpose(dst[0:XR, d * P:(d + 1) * P],
                                             parts[:, g * DP + d, :, :].rearrange("p a m -> p (a m)"),
                                             identb_sb[:, :])
                mm.then_inc(turned, 1)

            def sums(u, xp, c, dst):
                nc.tensor.matmul(dst[0:UK, :], sel1_sb[:, u, :], xp[:, c * CH:(c + 1) * CH],
                                 start=True, stop=True).then_inc(sums_done, 1)

            def layer1(chunk, u):
                pe.wait_ge(lo_done, UT * chunk + u + 1)
                if u == 0 and not (isinstance(chunk, int) and chunk == 0):
                    pe.wait_ge(l1_read, chunk)
                for k, (w, s) in enumerate(((w1_hi, sq_hi), (w1_lo, sq_hi), (w1_hi, sq_lo))):
                    mm = nc.tensor.matmul(l1out[:, :], w[:, u, :], s[:, u, :],
                                          start=(u == 0 and k == 0), stop=(u == UT - 1 and k == 2))
                mm.then_inc(l1_done, 1)

            def spread_tile(t, k, xp):
                for c in range(2):
                    mm = nc.tensor.matmul(spread[k % 2][:, c, :], sel2_sb[:, t, :],
                                          xp[:, c * CH:(c + 1) * CH], start=True, stop=True)
                mm.then_inc(spread_done, 1)

            def main(t, k, lo):
                for c in range(2):
                    mm = nc.tensor.matmul(lo[c * HALF:(c + 1) * HALF, :], w2_sb[:, t, :],
                                          prod[k % 2][:, c, :], start=(t == 0), stop=(t == T2 - 1))
                mm.then_inc(main_done, 1)

            def turn_embeddings(k):
                if k >= 2:
                    pe.wait_ge(xt_lo_done, k - 1)
                n = P if k < K1 - 1 else EMB_LAST
                for b in range(BT):
                    row = emb[:, b, :, :].rearrange("p m e -> p (m e)")
                    mm = nc.tensor.transpose(turn_banks[k % 2][0:n, b * P:(b + 1) * P],
                                             row[:, k * P:k * P + n], ident_sb[:, :])
                mm.then_inc(xt_done, 1)

            def pairs(b, last):
                for g in range(GP):
                    i = b * GP + g
                    end = last and g == GP - 1
                    nxt, after = x[(g + 1) % 4], x[(g + 2) % 4]
                    two_on = not (last and g >= 2)
                    for t in range(T2):
                        k = slot(g, t)
                        pe.wait_ge(prod_done, i * T2 + t + 1)
                        main(t, k, l2out[g % 2])
                        if t + 2 < T2:
                            spread_tile(t + 2, k + 2, x[g])
                        elif not end:
                            spread_tile(t + 2 - T2, k + 2, nxt)
                        if end:
                            if t in TURN_E:
                                if t == 0:
                                    pe.wait_ge(emb_in, ROWS_IN * BT - ROWS_FIRST)
                                    pe.wait_ge(hi_done, UT * 2 * NPAIR)
                                    pe.wait_ge(l1_read, 2 * NPAIR)
                                turn_embeddings(TURN_E.index(t))
                            continue
                        if t in L1_B:
                            layer1(2 * i + 3, L1_B.index(t))
                        if t in L1_A and two_on:
                            layer1(2 * i + 4, L1_A.index(t))
                        if t in SUMS_B:
                            u = SUMS_B.index(t)
                            pe.wait_ge(hi_done, UT * (2 * i + 3) + u)
                            sums(u, nxt, 1, stage)
                        if t == TURN_AT and two_on:
                            pe.wait_ge(split_step, 4 * (b + (1 if g < 2 else 2)))
                            pe.wait_ge(hi_done, UT * (2 * i + 4))
                            turn((g + 2) % 4, stage_bf)
                        if t in SUMS_A and two_on:
                            u = SUMS_A.index(t)
                            if u == 0:
                                pe.wait_ge(x_ready, i + 3)
                            else:
                                pe.wait_ge(hi_done, UT * (2 * i + 4) + u)
                            sums(u, after, 0, stage)

            pe.wait_ge(w1_in, 48)
            pe.wait_ge(w1_step, 2)
            for u in range(UT):
                mm = nc.tensor.matmul(l1out[0:M, 0:P], fix_sb[:, u, :], w1a_sb[:, u, :],
                                      start=(u == 0), stop=(u == UT - 1))
            mm.then_inc(fix_done, 1)
            pe.wait_ge(ident_in, 32)
            pe.wait_ge(first_split, 4)
            pe.wait_ge(split_step, 4)
            turn(0, stage_bf)
            turn(1, early_turn)
            pe.wait_ge(sel_in, 32)
            pe.wait_ge(x_ready, 1)
            for chunk in range(2):
                for u in range(UT):
                    sums(u, x[0], chunk, early_sums[chunk * UT + u])
            pe.wait_ge(w1_step, 5)
            for u in range(UT):
                layer1(0, u)
            pe.wait_ge(x_ready, 2)
            sums(0, x[1], 0, early_sums[2 * UT])
            layer1(1, 0)
            pe.wait_ge(hi_done, 4)
            spread_tile(0, 0, x[0])
            spread_tile(1, 1, x[0])
            for u in range(1, UT):
                layer1(1, u)
                pe.wait_ge(hi_done, 4 + u)
                sums(u, x[1], 0, early_sums[2 * UT + u])
            for u in range(UT):
                layer1(2, u)
            pe.wait_ge(w2_in, 16)

            with pe.Fori(0, BT - 1) as b:
                pairs(b, False)
            pairs(BT - 1, True)

            pe.wait_ge(piece_lo, PIECES)
            pe.wait_ge(dense_split, 2)
            pe.wait_ge(xt_lo_done, K1)
            n = 0
            for layer, (hi, lo, kt, xh, xl) in enumerate((
                    (m1_hi, m1_lo, K1, xt_hi, xt_lo), (m2_hi, m2_lo, K2, h1_hi, h1_lo),
                    (m3_hi, m3_lo, K3, h2_hi, h2_lo))):
                before = sum(MT[:layer])
                for mt in range(MT[layer]):
                    if n >= 2:
                        pe.wait_ge(tanh_done, n - 1)
                    for k in range(kt):
                        if layer and mt == 0:
                            pe.wait_ge(h_lo_done, before - kt + k + 1)
                        r = K1_LAST if layer == 0 and k == K1 - 1 else P
                        for j, (w, h) in enumerate(((hi, xh), (lo, xh), (hi, xl))):
                            mm = nc.tensor.matmul(MLP_BANKS[n % 2][:, :], w[0:r, k, mt * P:(mt + 1) * P],
                                                  h[0:r, k, :], start=(k == 0 and j == 0),
                                                  stop=(k == kt - 1 and j == 2))
                    mm.then_inc(mlp_done, 1)
                    n += 1
                if layer == 0:
                    pe.wait_ge(fold_step, 6)
                    pe.wait_ge(small_in, 16)
                    pe.wait_ge(dense_in, 16)
                    pe.wait_ge(res2_ready, NPAIR + 1)
                    row = row_ps[0:1, :]
                    nc.tensor.matmul(row, small_sb[:, C_AUX:C_AUX + 1], aux[:, :], start=True, stop=False)
                    for c, f in ((C_CIN1, fold1), (C_CIN2, fold2)):
                        nc.tensor.matmul(row, small_sb[:, c:c + 1], f[:, :, :].rearrange("p t b -> p (t b)"),
                                         start=False, stop=False)
                    for t in range(BT):
                        nc.tensor.matmul(row_ps[0:1, t * P:(t + 1) * P], lin[:, t:t + 1], ident_sb[:, :],
                                         start=False, stop=False, skip_group_check=True)
            for k in range(D3 // P):
                pe.wait_ge(tanh_done, HT - D3 // P + k + 1)
                mm = nc.tensor.matmul(row_ps[0:1, :], small_sb[:, C_DEEP + k:C_DEEP + k + 1], h3[:, k, :],
                                      start=False, stop=(k == D3 // P - 1))
            mm.then_inc(row_done, 1)

        @block.scalar
        def _(act):
            def copy_x(pair, k):
                act.wait_ge(turned, pair + 1)
                nc.scalar.activation(x[k][:, :], stage_bf[0:XR, :], ACT.Copy).then_inc(x_ready, 1)

            def squares(chunk, u, src=stage):
                act.wait_ge(sums_done, chunk * UT + u + 1)
                if not (isinstance(chunk, int) and chunk == 0):
                    act.wait_ge(l1_done, (chunk - 1) * UT + u + 1)
                nc.scalar.activation(sq[:, u, :], src[0:UK, :], ACT.Square)
                nc.scalar.activation(sq_hi[:, u, :], src[0:UK, :], ACT.Square).then_inc(hi_done, 1)

            def sigmoid(chunk, c, k, q):
                if q == 0:
                    act.wait_ge(l1_done, UT * (chunk + 1))
                if q < 2:
                    nc.scalar.activation(xk[k][q * HALF:(q + 1) * HALF, c, :], l1out[0:HALF, :], ACT.Sigmoid,
                                         bias=small_sb[0:HALF, C_CB1:C_CB1 + 1]).then_inc(xk_ready, 1)
                else:
                    nc.scalar.activation(res1[k][c * HALF:(c + 1) * HALF, :], l1out[HALF:P, :], ACT.Sigmoid,
                                         bias=small_sb[HALF:P, C_CB1:C_CB1 + 1]).then_inc(l1_read, 1)

            def pairs(b, last):
                for g in range(GP):
                    i = b * GP + g
                    end = last and g == GP - 1
                    if not end:
                        for u in range(UT):
                            squares(2 * i + 3, u)
                            if u == 0:
                                act.wait_ge(prod_done, i * T2 + 1)
                            sigmoid(2 * i + 2, 0, (g + 1) % 2, u)
                        two_on = not (last and g >= 2)
                        if two_on:
                            copy_x(i + 2, (g + 2) % 4)
                        for u in range(UT):
                            if two_on:
                                squares(2 * i + 4, u)
                            sigmoid(2 * i + 3, 1, (g + 1) % 2, u)
                    else:
                        act.wait_ge(dense_in, 16)
                        nc.scalar.activation(xt_hi[DENSE_AT:K1_LAST, K1 - 1, :],
                                             aux[DENSE_AT:K1_LAST, :], ACT.Copy).then_inc(dense_split, 1)
                        for k in range(K1):
                            n = P if k < K1 - 1 else EMB_LAST
                            act.wait_ge(xt_done, k + 1)
                            if k == K1 - 1:
                                act.wait_ge(pad_done, 2)
                            nc.scalar.activation(xt_hi[0:n, k, :], turn_banks[k % 2][0:n, :], ACT.Copy)\
                              .then_inc(xt_hi_done, 1)
                    act.wait_ge(main_done, (i + 1) * T2)
                    nc.scalar.activation(res2[g % 2][:, :], l2out[g % 2][:, :], ACT.Sigmoid,
                                         bias=small_sb[:, C_CB2:C_CB2 + 1]).then_inc(res2_ready, 1)

            act.wait_ge(zeroed, 1)
            nc.scalar.activation(res1[0][0:1, 0:1], aux[0:1, 0:1], ACT.Sigmoid)
            copy_x(0, 0)
            act.wait_ge(small_in, 16)
            for u in range(UT):
                squares(0, u, early_sums[u])
            for chunk in range(2):
                for u in range(UT):
                    if u == UT - 1:
                        for q in range(3):
                            sigmoid(chunk, chunk, 0, q)
                    squares(chunk + 1, u, early_sums[(chunk + 1) * UT + u])

            with act.Fori(0, BT - 1) as b:
                pairs(b, False)
            pairs(BT - 1, True)

            n = 0
            for layer, bias in enumerate((C_B1, C_B2, C_B3)):
                for mt in range(MT[layer]):
                    act.wait_ge(mlp_done, n + 1)
                    if layer < 2 and n >= 2:
                        act.wait_ge(h_lo_done, n - 1)
                    dst = hf[n % 2] if layer < 2 else h3[:, mt, :]
                    nc.scalar.activation(dst, MLP_BANKS[n % 2][:, :], ACT.Tanh,
                                         bias=small_sb[:, bias + mt:bias + mt + 1]).then_inc(tanh_done, 1)
                    n += 1

        @block.vector
        def _(dve):
            def split(b, step, m0=0, m1=M, done=split_step):
                e = emb[:, bass.ds(b, 1), m0:m1, 0:E].rearrange("p t m d -> p (t m) d") \
                    if not isinstance(b, int) else emb[:, b, m0:m1, 0:E]
                part = [parts[:, :, j, m0:m1].rearrange("p d m -> p m d") for j in range(3)]
                left = rest[:, m0:m1, :]
                if step == 0:
                    ins = nc.vector.tensor_copy(part[0], e)
                elif step == 1:
                    ins = nc.vector.tensor_tensor(left, e, part[0], ALU.subtract)
                elif step == 2:
                    ins = nc.vector.tensor_copy(part[1], left)
                else:
                    ins = nc.vector.tensor_tensor(part[2], left, part[1], ALU.subtract)
                ins.then_inc(done, 1)

            def low(tile, u):
                dve.wait_ge(hi_done, tile + 1)
                nc.vector.tensor_tensor(sq_lo[:, u, :], sq[:, u, :], sq_hi[:, u, :].bitcast(F32),
                                        ALU.subtract).then_inc(lo_done, 1)

            def block_of(a, b, off):
                if isinstance(b, int):
                    return a[:, b + off, :]
                return a[:, bass.ds(b + off, 1), :].rearrange("p t n -> p (t n)")

            def pairs(b, last):
                for g in range(GP):
                    i = b * GP + g
                    end = last and g == GP - 1
                    for t in range(T2):
                        k = slot(g, t)
                        dve.wait_ge(spread_done, i * T2 + t + 1)
                        if t == 0:
                            dve.wait_ge(xk_ready, 4 * (i + 1))
                        nc.vector.tensor_tensor(prod[k % 2][:, :, :].rearrange("p c n -> p (c n)"),
                                                spread[k % 2][:, :, :].rearrange("p c n -> p (c n)"),
                                                xk[g % 2][:, :, :].rearrange("p c n -> p (c n)"),
                                                ALU.mult).then_inc(prod_done, 1)
                        if t in LOW_B and not end:
                            u = LOW_B.index(t)
                            low(UT * (2 * i + 3) + u, u)
                        if t in LOW_A and not (last and g >= 2):
                            u = LOW_A.index(t)
                            low(UT * (2 * i + 4) + u, u)
                        if t == ADD1_AT:
                            dve.wait_ge(l1_read, 2 * (i + 1))
                            a = block_of(acc1, b, 0)
                            nc.vector.tensor_tensor(a, a, res1[g % 2][:, :], ALU.add).then_inc(add1_done, 1)
                        if t == ADD2_AT:
                            dve.wait_ge(res2_ready, i + 1)
                            a = block_of(acc2, b, 0 if g == 0 else 1)
                            nc.vector.tensor_tensor(a, a, res2[(g + 1) % 2][:, :], ALU.add)\
                              .then_inc(add2_done, 1)
                        if g == 1 and not last and t in SPLIT_AT:
                            step = SPLIT_AT.index(t)
                            if step == 0:
                                dve.wait_ge(emb_in, ROWS_IN * (b + 2) - ROWS_FIRST)
                                dve.wait_ge(turned, 4 * (b + 1))
                            else:
                                dve.wait_ge(split_step, 4 * (b + 1) + step)
                            split(b + 1, step)
                        if end and t == 0:
                            dve.wait_ge(dense_split, 1)
                            nc.vector.tensor_tensor(xt_lo[DENSE_AT:K1_LAST, K1 - 1, :],
                                                    aux[DENSE_AT:K1_LAST, :],
                                                    xt_hi[DENSE_AT:K1_LAST, K1 - 1, :].bitcast(F32),
                                                    ALU.subtract).then_inc(dense_split, 1)
                        if end and t - 1 in TURN_E:
                            tile = TURN_E.index(t - 1)
                            n = P if tile < K1 - 1 else EMB_LAST
                            dve.wait_ge(xt_hi_done, tile + 1)
                            if tile == K1 - 1:
                                dve.wait_ge(pad_done, 2)
                            nc.vector.tensor_tensor(xt_lo[0:n, tile, :], turn_banks[tile % 2][0:n, :],
                                                    xt_hi[0:n, tile, :].bitcast(F32), ALU.subtract)\
                              .then_inc(xt_lo_done, 1)

            dve.wait_ge(idx_in, 16)
            nc.vector.tensor_scalar(wrap[:, :, :], idx_sb[:, :, :], 0.0, float(V), ALU.is_lt, ALU.mult)\
              .then_inc(idx_step, 1)
            dve.wait_ge(idx_step, 1)
            nc.vector.tensor_tensor(inside[:, :, :], idx_sb[:, :, :], wrap[:, :, :], ALU.add).then_inc(idx_step, 1)
            dve.wait_ge(idx_step, 2)
            nc.vector.tensor_scalar(clamped[:, :, :], inside[:, :, :], 0.0, float(V - 1), ALU.max, ALU.min)\
              .then_inc(idx_step, 1)
            dve.wait_ge(base_in, 16)
            dve.wait_ge(idx_step, 3)
            nc.vector.tensor_tensor(rows[:, :, :], clamped[:, :, :], base_sb[:, :, :], ALU.add).then_inc(idx_step, 2)
            nc.vector.memset(aux[:, :], 1.0).then_inc(zeroed, 1)
            nc.vector.memset(acc1[:, :, :], 0.0).then_inc(zeroed, 1)
            nc.vector.memset(acc2[:, :, :], 0.0).then_inc(zeroed, 1)
            nc.vector.memset(res2[1][:, :], 0.0).then_inc(res2_ready, 1)
            dve.wait_ge(w1_in, 48)
            nc.vector.tensor_tensor(w1b_sb[:, :, :], w1a_sb[:, :, :], w1b_sb[:, :, :], ALU.add).then_inc(w1_step, 1)
            dve.wait_ge(w1_step, 1)
            nc.vector.tensor_scalar(w1a_sb[:, :, :], w1b_sb[:, :, :], 0.5, None, ALU.mult).then_inc(w1_step, 1)
            dve.wait_ge(fix_done, 1)
            nc.vector.tensor_copy(w1a_sb[0:M, 0, :], l1out[0:M, 0:P]).then_inc(w1_step, 1)
            dve.wait_ge(w1_step, 3)
            nc.vector.tensor_copy(w1_hi[:, :, :], w1a_sb[:, :, :]).then_inc(w1_step, 1)
            dve.wait_ge(w1_step, 4)
            nc.vector.tensor_tensor(w1_lo[:, :, :], w1a_sb[:, :, :], w1_hi[:, :, :].bitcast(F32),
                                    ALU.subtract).then_inc(w1_step, 1)
            dve.wait_ge(zeroed, 3)
            for m0, m1, rows_in, n, done in ((0, FIRST, first_in, FIRST, first_split),
                                             (FIRST, M, emb_in, M - FIRST, split_step)):
                dve.wait_ge(rows_in, 16 * n)
                for step in range(4):
                    if step:
                        dve.wait_ge(done, step)
                    split(0, step, m0, m1, done)
            dve.wait_ge(turned, 2)
            dve.wait_ge(x_ready, 1)
            nc.vector.tensor_copy(x[1][:, :], early_turn[0:XR, :]).then_inc(x_ready, 1)
            for tile in range(3 * UT):
                low(tile, tile % UT)

            with dve.Fori(0, BT - 1) as b:
                pairs(b, False)
            pairs(BT - 1, True)

            nc.vector.tensor_reduce(lin[:, :], emb[:, :, :, E], AX.X, ALU.add).then_inc(fold_step, 1)
            dve.wait_ge(res2_ready, NPAIR + 1)
            nc.vector.tensor_tensor(acc2[:, BT, :], acc2[:, BT, :], res2[1][:, :], ALU.add).then_inc(fold_step, 1)
            dve.wait_ge(add1_done, NPAIR)
            dve.wait_ge(fold_step, 2)
            for a, f, n in ((acc1[:, :, :], fold1, 3), (acc2[:, 1:BT + 1, :], fold2, 5)):
                half = a[:, :, 0:2 * P]
                nc.vector.tensor_tensor(half, half, a[:, :, 2 * P:4 * P], ALU.add).then_inc(fold_step, 1)
                dve.wait_ge(fold_step, n)
                nc.vector.tensor_tensor(f[:, :, :], a[:, :, 0:P], a[:, :, P:2 * P], ALU.add)\
                  .then_inc(fold_step, 1)

            n = 0
            for layer, (hi, lo) in enumerate(((h1_hi, h1_lo), (h2_hi, h2_lo))):
                for mt in range(MT[layer]):
                    dve.wait_ge(tanh_done, n + 1)
                    if layer and mt == 0:
                        dve.wait_ge(mlp_done, MT[0])
                    nc.vector.tensor_copy(hi[:, mt, :], hf[n % 2]).then_inc(h_hi_done, 1)
                    dve.wait_ge(h_hi_done, n + 1)
                    nc.vector.tensor_tensor(lo[:, mt, :], hf[n % 2], hi[:, mt, :].bitcast(F32),
                                            ALU.subtract).then_inc(h_lo_done, 1)
                    n += 1
            dve.wait_ge(row_done, 1)
            nc.vector.tensor_copy(row_sb, row_ps[0:1, :]).then_inc(row_read, 1)


def kernel(r_dense, r_sparse, L0_rec_tables, L0_rec_lin_sparse_w, L0_rec_lin_dense_w, L0_rec_conv1_w,
           L0_rec_conv1_b, L0_rec_conv2_w, L0_rec_conv2_b, L0_rec_cin_w, L0_rec_cin_b, L0_rec_W1, L0_rec_b1,
           L0_rec_W2, L0_rec_b2, L0_rec_W3, L0_rec_b3, L0_rec_deep_w, L0_rec_deep_b, L0_rec_bias):
    import ml_dtypes
    import numpy as np
    import concourse.bacc as bacc
    from concourse.bass_utils import run_bass_kernel_spmd

    a = np.asarray
    f32, bf = np.float32, ml_dtypes.bfloat16
    first = np.array([m for m in range(M)] + [m for m in range(M) for n in range(m + 1, M)])
    second = np.array([m for m in range(M)] + [n for m in range(M) for n in range(m + 1, M)])
    tiles = lambda w: np.ascontiguousarray(w.reshape(UT, UK, -1).transpose(1, 0, 2))
    conv1 = a(L0_rec_conv1_w).reshape(P, M, M)
    conv2 = a(L0_rec_conv2_w)[HALF:].reshape(HALF, HALF, T2, 2)
    pair_of = np.arange(NPR)
    sel1 = np.zeros((3, M, NPR), bf)
    sel1[:, first, pair_of] = 1
    sel1[:, second, pair_of] = 1
    sel2 = np.zeros((3, M, T2, 2, HALF), bf)
    fix = np.zeros((NPR, M), f32)
    fix[pair_of, first] = -1
    fix[pair_of, second] = -1
    fix[np.arange(M), np.arange(M)] = 1
    for t in range(T2):
        for j in range(2):
            sel2[:, 2 * t + j, t, j, :] = 1
    small = np.zeros((P, C_END), f32)
    small[:, C_B1:C_B2] = a(L0_rec_b1).reshape(-1, P).T
    small[:, C_B2:C_B3] = a(L0_rec_b2).reshape(-1, P).T
    small[:, C_B3:C_DEEP] = a(L0_rec_b3).reshape(-1, P).T
    small[:, C_DEEP:C_CB1] = a(L0_rec_deep_w).reshape(-1, P).T
    small[:, C_CB1] = a(L0_rec_conv1_b)
    for j in range(2):
        small[j * HALF:(j + 1) * HALF, C_CB2] = a(L0_rec_conv2_b)[HALF:]
        small[j * HALF:(j + 1) * HALF, C_CIN1] = a(L0_rec_cin_w)[:HALF, 0]
        small[j * HALF:(j + 1) * HALF, C_CIN2] = a(L0_rec_cin_w)[HALF:, 0]
    small[0, C_AUX], small[1, C_AUX], small[2, C_AUX] = a(L0_rec_cin_b)[0], a(L0_rec_deep_b)[0], a(L0_rec_bias)[0]
    small[DENSE_AT:K1_LAST, C_AUX] = a(L0_rec_lin_dense_w)
    mlp1 = np.zeros((K1 * P, D1), f32)
    mlp1[:M * ROW].reshape(M, ROW, D1)[:, :E] = a(L0_rec_W1)[:M * E].reshape(M, E, D1)
    mlp1[(K1 - 1) * P + DENSE_AT:(K1 - 1) * P + K1_LAST] = a(L0_rec_W1)[M * E:]

    arrays = {
        "idx": a(r_sparse),
        "idx_base": np.ascontiguousarray(np.broadcast_to(np.arange(M, dtype=np.int32) * V, (P, BT, M))),
        "table": np.concatenate([a(L0_rec_tables), a(L0_rec_lin_sparse_w)[:, :, None]], axis=2).reshape(M * V, ROW),
        "dense_t": np.ascontiguousarray(a(r_dense).T),
        "w1a": tiles(conv1[:, first, second].T),
        "w1b": tiles(conv1[:, second, first].T),
        "w1_fix": tiles(fix),
        "w2": np.ascontiguousarray(conv2.transpose(3, 1, 2, 0).reshape(P, T2, HALF)),
        "mlp1": mlp1, "mlp2": a(L0_rec_W2), "mlp3": a(L0_rec_W3),
        "small": small,
        "sel1": np.ascontiguousarray(sel1.reshape(XR, UT, UK)),
        "sel2": np.ascontiguousarray(sel2.reshape(XR, T2, P)),
        "ident": np.eye(P, dtype=f32),
        "ident_bf": np.eye(P, dtype=f32).astype(bf),
    }
    nc = bacc.Bacc("TRN2", target_bir_lowering=False, num_devices=1)
    args = {k: nc.dram_tensor(f"in_{k}", v.shape, mybir.dt.from_np(v.dtype), kind="ExternalInput").ap()
            for k, v in arrays.items()}
    out = nc.dram_tensor("out_row", (B,), F32, kind="ExternalOutput").ap()
    build(nc, out=out, **args)
    r = run_bass_kernel_spmd(nc, [{f"in_{k}": v for k, v in arrays.items()}], core_ids=[0])
    return r.results[0]["out_row"]
```
